# Optimizing a Trainium2 kernel written in Bass

```python
import numpy as np
import jax
import jax.numpy as jnp

def _softmax(x, axis=-1):
    return jax.nn.softmax(x, axis=axis)

def _gelu(x):
    return jax.nn.gelu(x, approximate=True)

def _silu(x):
    return jax.nn.silu(x)

def _sigmoid(x):
    return jax.nn.sigmoid(x)

def _layernorm(x, axis=-1, eps=1e-05):
    m = jnp.mean(x, axis=axis, keepdims=True)
    v = jnp.var(x, axis=axis, keepdims=True)
    return (x - m) / jnp.sqrt(v + eps)

def _scatter_add(tgt, idx, src, axis=0):
    return tgt.at[idx].add(src)

def _segment_sum(src, seg, n):
    return jax.ops.segment_sum(src, seg, n)
kernel_name = 'mk_rec_standalone_d1_rec_r8_ea4ed2'

def setup_inputs(seed: int=0):
    np.random.seed(seed)
    _w = jnp.asarray

    def _rec_inputs():
        import jax
        import jax.numpy as jnp
        _rk = jax.random.key(seed)
        r_item_emb_d128 = 0.000227908 + 0.99994 * jax.random.normal(jax.random.fold_in(_rk, 1), (512, 128), jnp.float32)
        r_item_id = jax.random.randint(jax.random.fold_in(_rk, 2), (512,), 4, 91707, jnp.int32)
        r_likes_level = jax.random.randint(jax.random.fold_in(_rk, 3), (512,), 0, 11, jnp.int32)
        r_views_level = jax.random.randint(jax.random.fold_in(_rk, 4), (512,), 0, 11, jnp.int32)
        r_item_seq = jnp.stack([jax.random.randint(jax.random.fold_in(jax.random.fold_in(_rk, 5), 0), (512,), 19, 91699, jnp.int32), jax.random.randint(jax.random.fold_in(jax.random.fold_in(_rk, 5), 1), (512,), 14, 91713, jnp.int32), jax.random.randint(jax.random.fold_in(jax.random.fold_in(_rk, 5), 2), (512,), 0, 11464, jnp.int32), jax.random.randint(jax.random.fold_in(jax.random.fold_in(_rk, 5), 3), (512,), 19, 91717, jnp.int32), jax.random.randint(jax.random.fold_in(jax.random.fold_in(_rk, 5), 4), (512,), 4, 91711, jnp.int32), jax.random.randint(jax.random.fold_in(jax.random.fold_in(_rk, 5), 5), (512,), 24, 91677, jnp.int32), jax.random.randint(jax.random.fold_in(jax.random.fold_in(_rk, 5), 6), (512,), 14, 91711, jnp.int32), jax.random.randint(jax.random.fold_in(jax.random.fold_in(_rk, 5), 7), (512,), 2, 91700, jnp.int32), jax.random.randint(jax.random.fold_in(jax.random.fold_in(_rk, 5), 8), (512,), 2, 91718, jnp.int32), jax.random.randint(jax.random.fold_in(jax.random.fold_in(_rk, 5), 9), (512,), 9, 91715, jnp.int32), jax.random.randint(jax.random.fold_in(jax.random.fold_in(_rk, 5), 10), (512,), 7, 91714, jnp.int32), jax.random.randint(jax.random.fold_in(jax.random.fold_in(_rk, 5), 11), (512,), 0, 91711, jnp.int32), jax.random.randint(jax.random.fold_in(jax.random.fold_in(_rk, 5), 12), (512,), 8, 91718, jnp.int32), jax.random.randint(jax.random.fold_in(jax.random.fold_in(_rk, 5), 13), (512,), 3, 91703, jnp.int32), jax.random.randint(jax.random.fold_in(jax.random.fold_in(_rk, 5), 14), (512,), 2, 91710, jnp.int32), jax.random.randint(jax.random.fold_in(jax.random.fold_in(_rk, 5), 15), (512,), 17, 91711, jnp.int32), jax.random.randint(jax.random.fold_in(jax.random.fold_in(_rk, 5), 16), (512,), 8, 91717, jnp.int32), jax.random.randint(jax.random.fold_in(jax.random.fold_in(_rk, 5), 17), (512,), 10, 91717, jnp.int32), jax.random.randint(jax.random.fold_in(jax.random.fold_in(_rk, 5), 18), (512,), 3, 91706, jnp.int32), jax.random.randint(jax.random.fold_in(jax.random.fold_in(_rk, 5), 19), (512,), 2, 91718, jnp.int32), jax.random.randint(jax.random.fold_in(jax.random.fold_in(_rk, 5), 20), (512,), 0, 91669, jnp.int32), jax.random.randint(jax.random.fold_in(jax.random.fold_in(_rk, 5), 21), (512,), 4, 91707, jnp.int32), jax.random.randint(jax.random.fold_in(jax.random.fold_in(_rk, 5), 22), (512,), 9, 91703, jnp.int32), jax.random.randint(jax.random.fold_in(jax.random.fold_in(_rk, 5), 23), (512,), 32, 91694, jnp.int32), jax.random.randint(jax.random.fold_in(jax.random.fold_in(_rk, 5), 24), (512,), 27, 91693, jnp.int32), jax.random.randint(jax.random.fold_in(jax.random.fold_in(_rk, 5), 25), (512,), 1, 11463, jnp.int32), jax.random.randint(jax.random.fold_in(jax.random.fold_in(_rk, 5), 26), (512,), 25, 91718, jnp.int32), jax.random.randint(jax.random.fold_in(jax.random.fold_in(_rk, 5), 27), (512,), 9, 91718, jnp.int32), jax.random.randint(jax.random.fold_in(jax.random.fold_in(_rk, 5), 28), (512,), 30, 91708, jnp.int32), jax.random.randint(jax.random.fold_in(jax.random.fold_in(_rk, 5), 29), (512,), 1, 91694, jnp.int32), jax.random.randint(jax.random.fold_in(jax.random.fold_in(_rk, 5), 30), (512,), 1, 91715, jnp.int32), jax.random.randint(jax.random.fold_in(jax.random.fold_in(_rk, 5), 31), (512,), 12, 91674, jnp.int32), jax.random.randint(jax.random.fold_in(jax.random.fold_in(_rk, 5), 32), (512,), 21, 91702, jnp.int32), jax.random.randint(jax.random.fold_in(jax.random.fold_in(_rk, 5), 33), (512,), 5, 91716, jnp.int32), jax.random.randint(jax.random.fold_in(jax.random.fold_in(_rk, 5), 34), (512,), 1, 91710, jnp.int32), jax.random.randint(jax.random.fold_in(jax.random.fold_in(_rk, 5), 35), (512,), 3, 91714, jnp.int32), jax.random.randint(jax.random.fold_in(jax.random.fold_in(_rk, 5), 36), (512,), 23, 11462, jnp.int32), jax.random.randint(jax.random.fold_in(jax.random.fold_in(_rk, 5), 37), (512,), 6, 91706, jnp.int32), jax.random.randint(jax.random.fold_in(jax.random.fold_in(_rk, 5), 38), (512,), 7, 91706, jnp.int32), jax.random.randint(jax.random.fold_in(jax.random.fold_in(_rk, 5), 39), (512,), 23, 91705, jnp.int32), jax.random.randint(jax.random.fold_in(jax.random.fold_in(_rk, 5), 40), (512,), 21, 91702, jnp.int32), jax.random.randint(jax.random.fold_in(jax.random.fold_in(_rk, 5), 41), (512,), 7, 91714, jnp.int32), jax.random.randint(jax.random.fold_in(jax.random.fold_in(_rk, 5), 42), (512,), 9, 91711, jnp.int32), jax.random.randint(jax.random.fold_in(jax.random.fold_in(_rk, 5), 43), (512,), 15, 91702, jnp.int32), jax.random.randint(jax.random.fold_in(jax.random.fold_in(_rk, 5), 44), (512,), 0, 91716, jnp.int32), jax.random.randint(jax.random.fold_in(jax.random.fold_in(_rk, 5), 45), (512,), 8, 91713, jnp.int32), jax.random.randint(jax.random.fold_in(jax.random.fold_in(_rk, 5), 46), (512,), 5, 91715, jnp.int32), jax.random.randint(jax.random.fold_in(jax.random.fold_in(_rk, 5), 47), (512,), 28, 91710, jnp.int32), jax.random.randint(jax.random.fold_in(jax.random.fold_in(_rk, 5), 48), (512,), 0, 91699, jnp.int32), jax.random.randint(jax.random.fold_in(jax.random.fold_in(_rk, 5), 49), (512,), 43, 91689, jnp.int32)], axis=1)
        return (r_item_emb_d128, r_item_id, r_likes_level, r_views_level, r_item_seq)
    r_item_emb_d128, r_item_id, r_likes_level, r_views_level, r_item_seq = _rec_inputs()

    def _L0_rec_setup():
        import jax, jax.numpy as jnp
        import numpy as np
        EMB = 128
        NUM_FIELDS = 5
        TOTAL_DIM = (NUM_FIELDS + NUM_FIELDS * (NUM_FIELDS - 1) // 2) * EMB

        def _ln(x, g, b, eps=1e-05):
            m = jnp.mean(x, axis=-1, keepdims=True)
            v = jnp.mean(jnp.square(x - m), axis=-1, keepdims=True)
            return (x - m) * jax.lax.rsqrt(v + eps) * g + b

        def _forward(item_id, item_emb_d128, likes_level, views_level, item_seq, item_table, cate_table, mm_w, mm_b, mm_ln_g, mm_ln_b, aw1, ab1, aw2, ab2, se_w1, se_b1, se_w2, se_b2, bil_W, cross_K, cross_bias, w1, b1, ln1g, ln1b, w2, b2, ln2g, ln2b, w3, b3):
            B = item_id.shape[0]
            like_feat = cate_table[likes_level]
            view_feat = cate_table[views_level]
            item_id_feat = item_table[item_id]
            item_img_feat = jax.nn.gelu(_ln(item_emb_d128 @ mm_w + mm_b, mm_ln_g, mm_ln_b), approximate=False)
            target = item_id_feat + item_img_feat
            seq_emb = item_table[item_seq]
            mask = item_seq == 0
            t = jnp.broadcast_to(target[:, None, :], seq_emb.shape)
            x = jnp.concatenate([t, seq_emb, t - seq_emb, t * seq_emb], axis=-1)
            scores = (jax.nn.relu(x @ aw1 + ab1) @ aw2 + ab2)[..., 0]
            scores = jnp.where(mask, -1000000000.0, scores)
            weights = jax.nn.softmax(scores, axis=1)
            hist_feat = jnp.einsum('bs,bsd->bd', weights, seq_emb)
            sparse = jnp.stack([like_feat, view_feat, item_id_feat, item_img_feat, hist_feat], axis=1)
            z = jnp.mean(sparse, axis=-1)
            w = jax.nn.sigmoid(jax.nn.relu(z @ se_w1 + se_b1) @ se_w2 + se_b2)
            se = sparse * w[:, :, None]
            vids = jnp.einsum('bfd,fde->bfe', se[:, :4], bil_W)
            p = [vids[:, i] * se[:, j] for i in range(4) for j in range(i + 1, 5)]
            bil = jnp.stack(p, axis=1)
            dnn_in = jnp.concatenate([se.reshape(B, -1), bil.reshape(B, -1)], axis=1)
            xc = dnn_in
            for i in range(2):
                xc = dnn_in * (xc @ cross_K[i] + cross_bias[i]) + xc
            h = jax.nn.gelu(_ln(xc @ w1 + b1, ln1g, ln1b), approximate=False)
            h = jax.nn.gelu(_ln(h @ w2 + b2, ln2g, ln2b), approximate=False)
            logits = h @ w3 + b3
            return jax.nn.sigmoid(logits)[:, 0]
        key = jax.random.key(seed)
        ks = jax.random.split(key, 32)
        B, S = (1024, 50)
        d = {}
        d['item_id'] = jax.random.randint(ks[0], (B,), 0, 91718)
        d['item_emb_d128'] = jax.random.normal(ks[1], (B, EMB), jnp.float32)
        d['likes_level'] = jax.random.randint(ks[2], (B,), 0, 11)
        d['views_level'] = jax.random.randint(ks[3], (B,), 0, 11)
        d['item_seq'] = jax.random.randint(ks[4], (B, S), 0, 91718)
        d['item_table'] = (jax.random.normal(ks[5], (91718, EMB), jnp.float32) * 0.02).at[0].set(0.0)
        d['cate_table'] = jax.random.normal(ks[6], (11, EMB), jnp.float32) * 0.02
        d['mm_w'] = jax.random.normal(ks[7], (EMB, EMB), jnp.float32) * 0.05
        d['mm_b'] = jnp.zeros((EMB,), jnp.float32)
        d['mm_ln_g'] = jnp.ones((EMB,), jnp.float32)
        d['mm_ln_b'] = jnp.zeros((EMB,), jnp.float32)
        d['aw1'] = jax.random.normal(ks[8], (4 * EMB, 64), jnp.float32) * 0.04
        d['ab1'] = jnp.zeros((64,), jnp.float32)
        d['aw2'] = jax.random.normal(ks[9], (64, 1), jnp.float32) * 0.1
        d['ab2'] = jnp.zeros((1,), jnp.float32)
        d['se_w1'] = jax.random.normal(ks[10], (5, 2), jnp.float32) * 0.4
        d['se_b1'] = jnp.zeros((2,), jnp.float32)
        d['se_w2'] = jax.random.normal(ks[11], (2, 5), jnp.float32) * 0.4
        d['se_b2'] = jnp.zeros((5,), jnp.float32)
        d['bil_W'] = jax.random.normal(ks[12], (4, EMB, EMB), jnp.float32) * 0.09
        d['cross_K'] = jax.random.normal(ks[13], (2, TOTAL_DIM, TOTAL_DIM), jnp.float32) * 0.023
        d['cross_bias'] = jnp.zeros((2, TOTAL_DIM), jnp.float32)
        d['w1'] = jax.random.normal(ks[14], (TOTAL_DIM, 512), jnp.float32) * 0.02
        d['b1'] = jnp.zeros((512,), jnp.float32)
        d['ln1g'] = jnp.ones((512,), jnp.float32)
        d['ln1b'] = jnp.zeros((512,), jnp.float32)
        d['w2'] = jax.random.normal(ks[15], (512, 256), jnp.float32) * 0.04
        d['b2'] = jnp.zeros((256,), jnp.float32)
        d['ln2g'] = jnp.ones((256,), jnp.float32)
        d['ln2b'] = jnp.zeros((256,), jnp.float32)
        d['w3'] = jax.random.normal(ks[16], (256, 1), jnp.float32) * 0.06
        d['b3'] = jnp.zeros((1,), jnp.float32)
        return d
    _L0_rec_all = _L0_rec_setup()
    _L0_rec_in = {k: v for k, v in _L0_rec_all.items() if k in ('item_table', 'cate_table', 'mm_w', 'mm_b', 'mm_ln_g', 'mm_ln_b', 'aw1', 'ab1', 'aw2', 'ab2', 'se_w1', 'se_b1', 'se_w2', 'se_b2', 'bil_W', 'cross_K', 'cross_bias', 'w1', 'b1', 'ln1g', 'ln1b', 'w2', 'b2', 'ln2g', 'ln2b', 'w3', 'b3')}
    del _L0_rec_all
    return {'r_item_emb_d128': r_item_emb_d128, 'r_item_id': r_item_id, 'r_likes_level': r_likes_level, 'r_views_level': r_views_level, 'r_item_seq': r_item_seq, 'L0_rec_item_table': _L0_rec_in['item_table'], 'L0_rec_cate_table': _L0_rec_in['cate_table'], 'L0_rec_mm_w': _L0_rec_in['mm_w'], 'L0_rec_mm_b': _L0_rec_in['mm_b'], 'L0_rec_mm_ln_g': _L0_rec_in['mm_ln_g'], 'L0_rec_mm_ln_b': _L0_rec_in['mm_ln_b'], 'L0_rec_aw1': _L0_rec_in['aw1'], 'L0_rec_ab1': _L0_rec_in['ab1'], 'L0_rec_aw2': _L0_rec_in['aw2'], 'L0_rec_ab2': _L0_rec_in['ab2'], 'L0_rec_se_w1': _L0_rec_in['se_w1'], 'L0_rec_se_b1': _L0_rec_in['se_b1'], 'L0_rec_se_w2': _L0_rec_in['se_w2'], 'L0_rec_se_b2': _L0_rec_in['se_b2'], 'L0_rec_bil_W': _L0_rec_in['bil_W'], 'L0_rec_cross_K': _L0_rec_in['cross_K'], 'L0_rec_cross_bias': _L0_rec_in['cross_bias'], 'L0_rec_w1': _L0_rec_in['w1'], 'L0_rec_b1': _L0_rec_in['b1'], 'L0_rec_ln1g': _L0_rec_in['ln1g'], 'L0_rec_ln1b': _L0_rec_in['ln1b'], 'L0_rec_w2': _L0_rec_in['w2'], 'L0_rec_b2': _L0_rec_in['b2'], 'L0_rec_ln2g': _L0_rec_in['ln2g'], 'L0_rec_ln2b': _L0_rec_in['ln2b'], 'L0_rec_w3': _L0_rec_in['w3'], 'L0_rec_b3': _L0_rec_in['b3']}

def reference(r_item_emb_d128, r_item_id, r_likes_level, r_views_level, r_item_seq, L0_rec_item_table, L0_rec_cate_table, L0_rec_mm_w, L0_rec_mm_b, L0_rec_mm_ln_g, L0_rec_mm_ln_b, L0_rec_aw1, L0_rec_ab1, L0_rec_aw2, L0_rec_ab2, L0_rec_se_w1, L0_rec_se_b1, L0_rec_se_w2, L0_rec_se_b2, L0_rec_bil_W, L0_rec_cross_K, L0_rec_cross_bias, L0_rec_w1, L0_rec_b1, L0_rec_ln1g, L0_rec_ln1b, L0_rec_w2, L0_rec_b2, L0_rec_ln2g, L0_rec_ln2b, L0_rec_w3, L0_rec_b3):
    import jax
    import jax.numpy as jnp

    def _L0_rec_ref(item_id, item_emb_d128, likes_level, views_level, item_seq, item_table, cate_table, mm_w, mm_b, mm_ln_g, mm_ln_b, aw1, ab1, aw2, ab2, se_w1, se_b1, se_w2, se_b2, bil_W, cross_K, cross_bias, w1, b1, ln1g, ln1b, w2, b2, ln2g, ln2b, w3, b3):
        import jax, jax.numpy as jnp
        import numpy as np
        EMB = 128
        NUM_FIELDS = 5
        TOTAL_DIM = (NUM_FIELDS + NUM_FIELDS * (NUM_FIELDS - 1) // 2) * EMB

        def _ln(x, g, b, eps=1e-05):
            m = jnp.mean(x, axis=-1, keepdims=True)
            v = jnp.mean(jnp.square(x - m), axis=-1, keepdims=True)
            return (x - m) * jax.lax.rsqrt(v + eps) * g + b

        def _forward(item_id, item_emb_d128, likes_level, views_level, item_seq, item_table, cate_table, mm_w, mm_b, mm_ln_g, mm_ln_b, aw1, ab1, aw2, ab2, se_w1, se_b1, se_w2, se_b2, bil_W, cross_K, cross_bias, w1, b1, ln1g, ln1b, w2, b2, ln2g, ln2b, w3, b3):
            B = item_id.shape[0]
            like_feat = cate_table[likes_level]
            view_feat = cate_table[views_level]
            item_id_feat = item_table[item_id]
            item_img_feat = jax.nn.gelu(_ln(item_emb_d128 @ mm_w + mm_b, mm_ln_g, mm_ln_b), approximate=False)
            target = item_id_feat + item_img_feat
            seq_emb = item_table[item_seq]
            mask = item_seq == 0
            t = jnp.broadcast_to(target[:, None, :], seq_emb.shape)
            x = jnp.concatenate([t, seq_emb, t - seq_emb, t * seq_emb], axis=-1)
            scores = (jax.nn.relu(x @ aw1 + ab1) @ aw2 + ab2)[..., 0]
            scores = jnp.where(mask, -1000000000.0, scores)
            weights = jax.nn.softmax(scores, axis=1)
            hist_feat = jnp.einsum('bs,bsd->bd', weights, seq_emb)
            sparse = jnp.stack([like_feat, view_feat, item_id_feat, item_img_feat, hist_feat], axis=1)
            z = jnp.mean(sparse, axis=-1)
            w = jax.nn.sigmoid(jax.nn.relu(z @ se_w1 + se_b1) @ se_w2 + se_b2)
            se = sparse * w[:, :, None]
            vids = jnp.einsum('bfd,fde->bfe', se[:, :4], bil_W)
            p = [vids[:, i] * se[:, j] for i in range(4) for j in range(i + 1, 5)]
            bil = jnp.stack(p, axis=1)
            dnn_in = jnp.concatenate([se.reshape(B, -1), bil.reshape(B, -1)], axis=1)
            xc = dnn_in
            for i in range(2):
                xc = dnn_in * (xc @ cross_K[i] + cross_bias[i]) + xc
            h = jax.nn.gelu(_ln(xc @ w1 + b1, ln1g, ln1b), approximate=False)
            h = jax.nn.gelu(_ln(h @ w2 + b2, ln2g, ln2b), approximate=False)
            logits = h @ w3 + b3
            return jax.nn.sigmoid(logits)[:, 0]
        return _forward(item_id, item_emb_d128, likes_level, views_level, item_seq, item_table, cate_table, mm_w, mm_b, mm_ln_g, mm_ln_b, aw1, ab1, aw2, ab2, se_w1, se_b1, se_w2, se_b2, bil_W, cross_K, cross_bias, w1, b1, ln1g, ln1b, w2, b2, ln2g, ln2b, w3, b3)
    y = _L0_rec_ref(r_item_id, r_item_emb_d128, r_likes_level, r_views_level, r_item_seq, L0_rec_item_table, L0_rec_cate_table, L0_rec_mm_w, L0_rec_mm_b, L0_rec_mm_ln_g, L0_rec_mm_ln_b, L0_rec_aw1, L0_rec_ab1, L0_rec_aw2, L0_rec_ab2, L0_rec_se_w1, L0_rec_se_b1, L0_rec_se_w2, L0_rec_se_b2, L0_rec_bil_W, L0_rec_cross_K, L0_rec_cross_bias, L0_rec_w1, L0_rec_b1, L0_rec_ln1g, L0_rec_ln1b, L0_rec_w2, L0_rec_b2, L0_rec_ln2g, L0_rec_ln2b, L0_rec_w3, L0_rec_b3)
    return y

_drawn_inputs = setup_inputs


def setup_inputs(seed=0):
    import zlib

    import numpy as np

    out = dict(_drawn_inputs(seed))
    spreads = {'L0_rec_mm_b': (0.0, 0.1),
     'L0_rec_mm_ln_g': (1.0, 0.2),
     'L0_rec_mm_ln_b': (0.0, 0.1),
     'L0_rec_ab1': (0.0, 0.8),
     'L0_rec_se_b1': (0.0, 0.8),
     'L0_rec_se_b2': (0.0, 0.8),
     'L0_rec_cross_bias': (0.0, 0.1),
     'L0_rec_b1': (0.0, 0.1),
     'L0_rec_ln1g': (1.0, 0.2),
     'L0_rec_ln1b': (0.0, 0.288),
     'L0_rec_b2': (0.0, 0.1),
     'L0_rec_ln2g': (1.0, 0.2),
     'L0_rec_ln2b': (0.0, 0.357)}
    factors = {'L0_rec_item_table': 6.186,
     'L0_rec_cate_table': 4.528,
     'L0_rec_aw1': 8.0,
     'L0_rec_aw2': 8.0,
     'L0_rec_se_w1': 8.0,
     'L0_rec_se_w2': 8.0,
     'L0_rec_bil_W': 8.0}
    for name, (base, spread) in spreads.items():
        noise = np.random.default_rng([zlib.crc32(name.encode()), seed]).standard_normal(out[name].shape)
        drawn = base * np.exp(spread * noise) if base else spread * noise
        out[name] = jnp.asarray(drawn.astype(out[name].dtype))
    for name, factor in factors.items():
        out[name] = (out[name] * factor).astype(out[name].dtype)
    return out
```

```python
from contextlib import ExitStack

import concourse.bass as bass
from concourse import mybir

F32 = mybir.dt.float32
F32R = mybir.dt.float32r
I32 = mybir.dt.int32
ALU = mybir.AluOpType
ACT = mybir.ActivationFunctionType
AX_X = mybir.AxisListType.X

P = 128
BANK = 512
EPS = 1e-5
MASKED = -1000000000.0

INS = ['r_item_emb_d128', 'r_item_id', 'r_likes_level', 'r_views_level', 'r_item_seq',
       'L0_rec_item_table', 'L0_rec_cate_table', 'L0_rec_mm_w', 'L0_rec_mm_b', 'L0_rec_mm_ln_g',
       'L0_rec_mm_ln_b', 'L0_rec_aw1', 'L0_rec_ab1', 'L0_rec_aw2', 'L0_rec_ab2', 'L0_rec_se_w1',
       'L0_rec_se_b1', 'L0_rec_se_w2', 'L0_rec_se_b2', 'L0_rec_bil_W', 'L0_rec_cross_K',
       'L0_rec_cross_bias', 'L0_rec_w1', 'L0_rec_b1', 'L0_rec_ln1g', 'L0_rec_ln1b', 'L0_rec_w2',
       'L0_rec_b2', 'L0_rec_ln2g', 'L0_rec_ln2b', 'L0_rec_w3', 'L0_rec_b3']


class Steps:

    def __init__(self, eng, sem):
        self.eng, self.sem, self.n, self.i, self.per = eng, sem, 0, None, 0

    def done(self, instruction):
        instruction.then_inc(self.sem, 1)
        self.n += 1

    def wait(self, behind=0):
        n = self.n - behind
        self.eng.wait_ge(self.sem, n if self.i is None else self.i * self.per + n)

    def enter(self, i, per):
        self.i, self.per, self.start = i, per, self.n

    def leave(self, trips):
        assert self.n - self.start == self.per, (self.n - self.start, self.per)
        self.n = self.start + self.per * trips
        self.i = None


def build(nc, a, ident_in, iota_in, out):
    B, S = a['r_item_seq'].shape
    D = a['L0_rec_item_table'].shape[1]
    LV = a['L0_rec_cate_table'].shape[0]
    HID = a['L0_rec_aw1'].shape[1]
    NF, SE = a['L0_rec_se_w1'].shape
    NL, TD, _ = a['L0_rec_cross_K'].shape
    N1 = a['L0_rec_w1'].shape[1]
    N2 = a['L0_rec_w2'].shape[1]
    assert D == P and 2 * HID == P and B % (4 * P) == 0
    NT = B // P
    NG = NT // 2
    G = 2 * P
    CH = 10
    NC = S // CH
    CPG = 2 * NC
    HC = CH // 2
    KT = TD // P
    NV = NF - 1
    W1K = 3
    NW1 = KT // W1K
    K1 = N1 // P
    K2 = N2 // P
    ITEMS = NL * KT + NW1

    R_CB, R_G1 = 0, NL * KT
    R_B1 = R_G1 + K1
    R_G2 = R_B1 + K1
    R_B2 = R_G2 + K2
    R_MG = R_B2 + K2
    R_MB = R_MG + 1
    R_W3 = R_MB + 1
    R_AB1 = R_W3 + K2
    R_AW2 = R_AB1 + 1
    NR = R_AW2 + 2

    ctx = ExitStack()
    with ctx:
        def sb(name, shape, dt=F32, at=ctx):
            return at.enter_context(nc.sbuf_tensor(name, shape, dt))

        def ps(name, shape):
            return ctx.enter_context(nc.psum_tensor(name, shape, F32))

        def sem(name):
            return ctx.enter_context(nc.semaphore(name))

        HALF = 2 * KT * G
        with ExitStack() as early:
            used = [0]

            def eb(name, shape, dt=F32):
                n = 1
                for s in shape[1:]:
                    n *= s
                used[0] += n
                return sb(name, shape, dt, early)

            emb = eb("emb", [P, NT, D])
            emb_t = eb("emb_t", [P, NT, P])
            img_hat = eb("img_hat", [P, NT, D])
            id_rows = eb("id_rows", [P, NT, D])
            levels_i = eb("levels_i", [LV, 2, B], I32)
            levels_f = eb("levels_f", [LV, 2, B])
            one_hot = eb("one_hot", [LV, 2, B])
            vec_rows = eb("vec_rows", [NR, P])
            aw1 = eb("aw1", [P, 4, HID])
            mm_w = eb("mm_w", [P, D])
            cate = eb("cate", [LV, D])
            mm_b = eb("mm_b", [1, D])
            eb("fill_d", [P, HALF - used[0]])
            seq0 = eb("seq0", [P, S, D])
            s_t = eb("s_t", [P, CH * P])
            with ExitStack() as assembly:
                se = sb("se", [P, NF, G], F32, assembly)
                gate = sb("gate", [P, NF, G], F32, assembly)
                prod = sb("prod", [P, 2, NV * G], F32, assembly)
            with ExitStack() as mlp:
                hat1 = sb("hat1", [P, NT, N1], F32, mlp)
                h1_t = sb("h1_t", [P, K1, B], F32, mlp)
                hat2 = sb("hat2", [P, NT, N2], F32, mlp)
                h2_t = sb("h2_t", [P, K2, B], F32, mlp)
            eb("fill_x", [P, HALF])
            seq1 = eb("seq1", [P, S, D])
            p_t = eb("p_t", [P, CH * P])
            seq = [seq0, seq1]
        xd = sb("xd", [P, NG, 2, KT, G], F32R)
        xe = sb("xe", [P, NG, 2, KT, G], F32R)
        with ExitStack() as attention:
            target = sb("target", [P, B], F32, attention)
            u_neg = sb("u_neg", [P, B], F32, attention)
            act_h = sb("act_h", [P, HC * P], F32, attention)
        dn = sb("dn", [P, 2, B])
        xf = sb("xf", [P, 2, B])
        w_raw = sb("w_raw", [P, 2, KT * P])
        w_hi = sb("w_hi", [P, 2, KT * P], F32R)
        w_lo = sb("w_lo", [P, 2, KT * P], F32R)
        fields = sb("fields", [P, NF, B])
        ident = sb("ident", [P, P])
        iota = sb("iota", [LV, 1])
        vec = sb("vec", [P, NR])
        w_u = sb("w_u", [P, 2, HID])
        w_s = sb("w_s", [P, HID])
        w_p = sb("w_p", [P, HID])
        bil_w = sb("bil_w", [P, NV, D])
        w2 = sb("w2", [P, K1, N2])
        ones = sb("ones", [1, P])
        b1 = sb("b1", [1, N1])
        b2 = sb("b2", [1, N2])
        ab2 = sb("ab2", [P, 1])
        b3 = sb("b3", [1, 1])
        se1_in = sb("se1_in", [P, NF * SE])
        se1 = sb("se1", [P, NF * SE])
        se_b1 = sb("se_b1", [SE, 1])
        se2_in = sb("se2_in", [SE + 1, NF])
        se2 = sb("se2", [SE + 1, NF, P])
        squeeze = sb("squeeze", [SE + 1, G])
        idx = sb("idx", [P, NT, S], I32)
        idx_g = sb("idx_g", [P, 2, S], I32)
        ids = sb("ids", [P, NT], I32)
        kept = sb("kept", [P, NT, S])
        masked = sb("masked", [P, NT, S])
        c_row = sb("c_row", [P, NT])
        logit = sb("logit", [P, S])
        top = sb("top", [P, 1])
        exps = sb("exps", [P, S])
        total = sb("total", [P, 1])
        probs = sb("probs", [P, S])
        hist = sb("hist", [P, 2, D])
        stats = sb("stats", [P, NT, 6])
        moments = sb("moments", [P, NT, 2])
        spread = sb("spread", [P, NT])
        y = sb("y", [1, B])

        pT = ps("pT", [P, 3 * BANK])
        pH = ps("pH", [P, 2 * BANK])
        pM = ps("pM", [P, BANK])
        pA = ps("pA", [P, 2 * BANK])

        s_idx = sem("idx_loaded")
        s_small = sem("small_loaded")
        s_idr = sem("id_rows_landed")
        s_idxg = sem("idx_group_ready")
        s_seen = sem("idx_group_seen")
        s_rows = [sem(f"rows_landed{c}") for c in range(CPG)]
        s_raw = [sem(f"w_raw_landed{j}") for j in range(2)]
        s_out = sem("out_stored")
        s_vz = sem("vec_rows_zeroed")
        s_pro = sem("prologue_pe")
        s_pra = sem("prologue_act")
        s_dve = sem("dve_step")
        s_sqrt = sem("roots_taken")
        s_tr = sem("chunk_transposed")
        s_st = sem("s_t_ready")
        s_pt = sem("p_t_ready")
        s_h = sem("hidden_done")
        s_ah = sem("act_h_ready")
        s_sc = sem("scores_done")
        s_scf = [sem(f"scores_read{j}") for j in range(2)]
        s_top = sem("top_ready")
        s_exp = sem("exps_ready")
        s_prb = sem("probs_ready")
        s_hist = [sem(f"hist_ready{j}") for j in range(2)]
        s_ht = sem("hist_transposed")
        s_hc = sem("hist_copied")
        s_sq = sem("squeeze_summed")
        s_sqr = sem("squeeze_ready")
        s_ga = sem("gate_summed")
        s_gr = sem("gate_ready")
        s_se = sem("se_ready")
        s_vid = sem("vids_done")
        s_pr = sem("prod_ready")
        s_dh = sem("xd_hi_ready")
        s_dl = sem("xd_lo_ready")
        s_wh = sem("w_hi_ready")
        s_wl = sem("w_lo_ready")
        s_mm = sem("block_done")
        s_dn = sem("dn_ready")
        s_xf = [sem(f"xf_ready{j}") for j in range(2)]
        s_xh = sem("x_hi_ready")
        s_xl = sem("x_lo_ready")
        s_w1 = sem("w1_done")
        s_hat = sem("hats_ready")
        s_mt = sem("mlp_transposed")
        s_ge = sem("gelu_done")
        s_w2 = sem("w2_done")
        s_w3 = sem("w3_done")
        s_y = sem("y_ready")

        def f32(ap):
            return ap.bitcast(F32)

        def tiles(x, col, n):
            return x[:, bass.ds(col, n)]

        K = a['L0_rec_cross_K'].rearrange("l (k p) n -> l p k n", p=P)
        W1 = a['L0_rec_w1'].rearrange("(k p) n -> p k n", p=P)
        W2 = a['L0_rec_w2'].rearrange("(k p) n -> p k n", p=P)

        def row(name, n=1):
            return a[name].rearrange("(a n) -> a n", a=n)

        SMALL = []

        block = ctx.enter_context(nc.Block())

        @block.sync
        def _(sp):
            sp.dma_start(ids[:, :], a["r_item_id"].rearrange("(t p) -> p t", p=P), allow_slow_non_contiguous=True).then_inc(s_idx, 16)
            sp.dma_start(idx[:, :, :], a['r_item_seq'].rearrange("(t p) s -> p t s", p=P)).then_inc(s_idx, 16)

            def small(to, of):
                sp.dma_start(to, of).then_inc(s_small, 16)
                SMALL.append(1)

            small(ident[:, :], ident_in)
            small(emb[:, :, :], a['r_item_emb_d128'].rearrange("(t p) d -> p t d", p=P))
            small(mm_w[:, :], a['L0_rec_mm_w'])
            small(mm_b[:, :], row('L0_rec_mm_b'))
            small(iota[:, :], iota_in)
            small(cate[:, :], a['L0_rec_cate_table'])
            for j, name in enumerate(('r_likes_level', 'r_views_level')):
                small(levels_i[:, j, :], row(name).broadcast_to([LV, B]))
            small(aw1[:, :, :], a['L0_rec_aw1'].rearrange("(q p) n -> p q n", p=P))
            sp.wait_ge(s_vz, 1)
            small(vec_rows[R_CB:R_G1, :], a['L0_rec_cross_bias'].rearrange("l (m p) -> (l m) p", p=P))
            small(vec_rows[R_G1:R_B1, :], row('L0_rec_ln1g', K1))
            small(vec_rows[R_B1:R_G2, :], row('L0_rec_ln1b', K1))
            small(vec_rows[R_G2:R_B2, :], row('L0_rec_ln2g', K2))
            small(vec_rows[R_B2:R_MG, :], row('L0_rec_ln2b', K2))
            small(vec_rows[R_MG:R_MB, :], row('L0_rec_mm_ln_g'))
            small(vec_rows[R_MB:R_W3, :], row('L0_rec_mm_ln_b'))
            small(vec_rows[R_W3:R_AB1, :], a['L0_rec_w3'].rearrange("(c p) a -> c (p a)", p=P))
            for h in range(2):
                small(vec_rows[R_AB1:R_AB1 + 1, h * HID:(h + 1) * HID], row('L0_rec_ab1'))
                small(vec_rows[R_AW2 + h:R_AW2 + h + 1, h * HID:(h + 1) * HID],
                      a['L0_rec_aw2'].rearrange("p a -> a p"))
            small(ab2[:, :], row('L0_rec_ab2').broadcast_to([P, 1]))
            small(b3[:, :], row('L0_rec_b3'))
            small(se1_in[:, :], a['L0_rec_se_w1'].rearrange("(a f) i -> a (f i)", a=1).broadcast_to([P, NF * SE]))
            small(se_b1[:, :], a['L0_rec_se_b1'].rearrange("(p a) -> p a", a=1))
            small(se2_in[0:SE, :], a['L0_rec_se_w2'])
            small(se2_in[SE:SE + 1, :], row('L0_rec_se_b2'))
            small(bil_w[:, :, :], a['L0_rec_bil_W'].rearrange("f d e -> d f e"))
            small(w2[:, :, :], W2)
            small(b1[:, :], row('L0_rec_b1'))
            small(b2[:, :], row('L0_rec_b2'))

            raw3 = [w_raw[:, j, :].rearrange("p (k n) -> p k n", k=KT) for j in range(2)]
            for j in range(2):
                sp.dma_start(raw3[j], K[0, :, :, j * P:(j + 1) * P]).then_inc(s_raw[j], 16)
            for l in range(NL):
                first = 2 if l == 0 else 1
                if l:
                    sp.wait_ge(s_wl, KT - 1)
                    sp.dma_start(raw3[1], K[l, :, :, 0:P]).then_inc(s_raw[1], 16)
                with sp.Fori(0, (KT - first) // 2) as i:
                    for j in range(2):
                        sp.wait_ge(s_wl, 2 * i + l * KT + first + j - 1)
                        sp.dma_start(raw3[j], K[l, :, :, bass.ds(i * 2 * P + (first + j) * P, P)])\
                            .then_inc(s_raw[j], 16)
                if l == 0:
                    sp.wait_ge(s_wl, KT - 2)
                    sp.dma_start(raw3[0], K[0, :, :, (KT - 1) * P:KT * P]).then_inc(s_raw[0], 16)
            for q in range(NW1):
                n = NL * KT + q
                sp.wait_ge(s_wl, n - 1)
                sp.dma_start(w_raw[:, n % 2, 0:W1K * N1].rearrange("p (k n) -> p k n", k=W1K),
                             W1[:, q * W1K:(q + 1) * W1K, :]).then_inc(s_raw[n % 2], 16)
            sp.wait_ge(s_y, 1)
            sp.dma_start(out.rearrange("(a n) -> a n", a=1), y[:, :]).then_inc(s_out, 16)
            sp.wait_ge(s_out, 16)

        @block.gpsimd
        def _(pool):
            nc.gpsimd.memset(vec_rows[:, :], 0.0).then_inc(s_vz, 1)
            pool.wait_ge(s_idx, 32)
            table = a['L0_rec_item_table']
            for t in range(NT):
                nc.gpsimd.indirect_dma_start(
                    id_rows[:, t, :], None, table,
                    bass.IndirectOffsetOnAxis(ap=ids[:, t:t + 1], axis=0)).then_inc(s_idr, 16)
            with pool.Fori(0, NG) as g:
                for j in range(2):
                    pool.wait_ge(s_hist[j], g)
                    nc.gpsimd.tensor_copy(idx_g[:, j, :], idx[:, bass.ds(2 * g + j, 1), :].rearrange("p a s -> p (a s)"))\
                        .then_inc(s_idxg, 1)
                    pool.wait_ge(s_idxg, 2 * g + j + 1)
                    pool.sem_inc(s_seen, 1)
                    for s in range(S):
                        nc.gpsimd.indirect_dma_start(
                            seq[j][:, s, :], None, table,
                            bass.IndirectOffsetOnAxis(ap=idx_g[:, j, s:s + 1], axis=0))\
                            .then_inc(s_rows[j * NC + s // CH], 16)

            def whole(j, m, turn):
                pool.wait_ge(s_xf[j], turn)
                nc.gpsimd.tensor_tensor(
                    dn[:, j, :].rearrange("p (g n) -> p g n", g=NG),
                    f32(xd[:, :, 0, bass.ds(m, 1), :]).rearrange("p g a n -> p g (a n)"),
                    f32(xd[:, :, 1, bass.ds(m, 1), :]).rearrange("p g a n -> p g (a n)"),
                    ALU.add).then_inc(s_dn, 1)

            pool.wait_ge(s_dl, NG * NF)
            for l in range(NL):
                if l == 1:
                    whole(1, 0, KT // 2)
                if l == 0:
                    with pool.Fori(0, KT // 2) as i:
                        for j in range(2):
                            whole(j, 2 * i + j, i)
                    whole(0, KT - 1, KT // 2)
                else:
                    with pool.Fori(0, KT // 2) as i:
                        for j in range(2):
                            whole(j, 2 * i + 1 + j, i + (KT + 1) // 2)

        @block.scalar
        def _(act):
            act.wait_ge(s_pro, 1)
            nc.scalar.copy(vec[:, :], pM[:, 0:NR]).then_inc(s_pra, 1)
            nc.scalar.copy(emb_t[:, :, :], pT[:, 0:B]).then_inc(s_pra, 1)
            act.wait_ge(s_pro, 2)
            for j in range(2):
                nc.scalar.copy(fields[:, j, :], pT[:, (1 + j) * BANK:(1 + j) * BANK + B]).then_inc(s_pra, 1)
            act.wait_ge(s_dve, 11 + 2 * NT)
            nc.scalar.activation(spread[:, :], spread[:, :], ACT.Sqrt).then_inc(s_sqrt, 1)
            act.wait_ge(s_pro, 4)
            nc.scalar.copy(fields[:, 2, :], pT[:, 0:B]).then_inc(s_pra, 1)
            act.wait_ge(s_pro, 5)
            act.wait_ge(s_pra, 1)
            nc.scalar.activation(fields[:, 3, :], pT[:, BANK:BANK + B], ACT.Gelu,
                                 scale=vec[:, R_MG:R_MG + 1], bias=vec[:, R_MB:R_MB + 1]).then_inc(s_pra, 1)

            with act.Fori(0, NG) as g:
                for j in range(2):
                    for c in range(NC):
                        n = j * NC + c
                        act.wait_ge(s_tr, CPG * g + n + 1)
                        act.wait_ge(s_h, CPG * g + n)
                        nc.scalar.copy(s_t[:, :], pT[:, 0:CH * P]).then_inc(s_st, 1)
                    act.wait_ge(s_top, 2 * g + j + 1)
                    nc.scalar.activation(exps[:, :], logit[:, :], ACT.Exp, bias=top[:, 0:1],
                                         accum_out=total[:, 0:1]).then_inc(s_exp, 1)
                    act.wait_ge(s_ht, 2 * g + j + 1)
                    nc.scalar.copy(fields[:, 4, bass.ds(g * G + j * P, P)], pM[:, 384:384 + P]).then_inc(s_hc, 1)
                act.wait_ge(s_ga, g + 1)
                nc.scalar.activation(gate[:, :, :], pT[:, 0:NF * G].rearrange("p (f n) -> p f n", f=NF),
                                     ACT.Sigmoid).then_inc(s_gr, 1)
                act.wait_ge(s_se, g + 1)
                nc.scalar.copy(xd[:, bass.ds(g, 1), 0, 0:NF, :].rearrange("p a k n -> p (a k) n"),
                               se[:, :, :]).then_inc(s_dh, 1)
                at = NF
                for i in range(NV):
                    act.wait_ge(s_pr, NV * g + i + 1)
                    nc.scalar.copy(
                        xd[:, bass.ds(g, 1), 0, at:at + NV - i, :].rearrange("p a k n -> p (a k) n"),
                        prod[:, i % 2, 0:(NV - i) * G].rearrange("p (k n) -> p k n", n=G)).then_inc(s_dh, 1)
                    at += NV - i

            def split_w(j, n, turn, width=KT * P):
                act.wait_ge(s_raw[j], 16 * turn)
                act.wait_ge(s_mm, n - 1)
                nc.scalar.copy(w_hi[:, j, 0:width], w_raw[:, j, 0:width]).then_inc(s_wh, 1)

            def split_x(to, m, j, turn):
                act.wait_ge(s_xf[j], turn + 1)
                nc.scalar.copy(to[:, :, 0, bass.ds(m, 1), :].rearrange("p g a n -> p g (a n)"),
                               xf[:, j, :].rearrange("p (g n) -> p g n", g=NG)).then_inc(s_xh, 1)

            act.wait_ge(s_raw[0], 16)
            nc.scalar.copy(w_hi[:, 0, :], w_raw[:, 0, :]).then_inc(s_wh, 1)
            act.wait_ge(s_raw[1], 16)
            nc.scalar.copy(w_hi[:, 1, :], w_raw[:, 1, :]).then_inc(s_wh, 1)
            with act.Fori(0, KT // 2) as i:
                for j in range(2):
                    split_w(j, 2 * i + j + 2, i + 2)
                    split_x(xe, 2 * i + j, j, i)
            split_w(0, KT + 1, (KT + 1) // 2 + 1)
            split_x(xe, KT - 1, 0, KT // 2)
            split_w(1, KT + 2, (KT + 2) // 2 + 1, KT * P)
            split_x(xd, 0, 1, KT // 2)
            with act.Fori(0, KT // 2 - 1) as i:
                for j in range(2):
                    split_w(j, 2 * i + j + KT + 3, i + (KT + 3) // 2 + 1)
                    split_x(xd, 2 * i + 1 + j, j, i + (KT + 1) // 2)
            for n in range(NL * KT - 2, ITEMS - 2):
                split_w(n % 2, n + 2, (n + 2) // 2 + 1, W1K * N1)
                if n < NL * KT:
                    split_x(xd, n - KT, n % 2, n // 2)

            act.wait_ge(s_hat, 1)
            nc.scalar.activation(spread[:, :], spread[:, :], ACT.Sqrt).then_inc(s_sqrt, 1)
            for c in range(K1):
                act.wait_ge(s_mt, c + 1)
                nc.scalar.activation(h1_t[:, c, :], pM[:, :] if c % 2 else pH[:, BANK:2 * BANK], ACT.Gelu,
                                     scale=vec[:, R_G1 + c:R_G1 + c + 1],
                                     bias=vec[:, R_B1 + c:R_B1 + c + 1]).then_inc(s_ge, 1)
            act.wait_ge(s_hat, 3)
            nc.scalar.activation(spread[:, :], spread[:, :], ACT.Sqrt).then_inc(s_sqrt, 1)
            for c in range(K2):
                act.wait_ge(s_mt, K1 + c + 1)
                nc.scalar.activation(h2_t[:, c, :], pT[:, c * BANK:(c + 1) * BANK], ACT.Gelu,
                                     scale=vec[:, R_G2 + c:R_G2 + c + 1],
                                     bias=vec[:, R_B2 + c:R_B2 + c + 1]).then_inc(s_ge, 1)
            act.wait_ge(s_w3, 1)
            nc.scalar.activation(y[:, :], pH[0:1, 0:B], ACT.Sigmoid, bias=b3[0:1, 0:1]).then_inc(s_y, 1)

        @block.vector
        def _(dve):
            v = Steps(dve, s_dve)
            v.done(nc.vector.memset(ones[:, :], 1.0))
            v.done(nc.vector.memset(squeeze[:, :], 1.0))
            dve.wait_ge(s_idx, 32)
            v.done(nc.vector.tensor_scalar(kept[:, :, :], idx[:, :, :], 0.0, None, ALU.not_equal))
            v.done(nc.vector.tensor_scalar(masked[:, :, :], idx[:, :, :], 0.0, MASKED, ALU.is_equal, ALU.mult))
            dve.wait_ge(s_small, 16 * len(SMALL))
            v.done(nc.vector.tensor_copy(levels_f[:, :, :], levels_i[:, :, :]))
            v.wait()
            v.done(nc.vector.tensor_scalar(one_hot[:, :, :], levels_f[:, :, :], iota[:, 0:1], None, ALU.is_equal))
            for h in range(2):
                v.done(nc.vector.tensor_tensor(w_u[:, h, :], aw1[:, 0, :], aw1[:, 2, :], ALU.add))
            v.done(nc.vector.tensor_tensor(w_s[:, :], aw1[:, 1, :], aw1[:, 2, :], ALU.subtract))
            v.done(nc.vector.tensor_copy(w_p[:, :], aw1[:, 3, :]))
            assert v.n == 10
            dve.wait_ge(s_pro, 3)
            for t in range(NT):
                v.done(nc.vector.bn_stats(stats[:, t, :], pH[:, t * D:(t + 1) * D]))
            v.wait()
            for t in range(NT):
                v.done(nc.vector.bn_aggr(moments[:, t, :], stats[:, t, :]))
            v.wait()
            v.done(nc.vector.tensor_scalar(spread[:, :], moments[:, :, 1], EPS, None, ALU.add))
            assert v.n == 11 + 2 * NT
            dve.wait_ge(s_sqrt, 1)
            v.done(nc.vector.reciprocal(spread[:, :], spread[:, :]))
            v.wait()
            for t in range(NT):
                v.done(nc.vector.tensor_scalar(img_hat[:, t, :], pH[:, t * D:(t + 1) * D], moments[:, t, 0:1],
                                               spread[:, t:t + 1], ALU.subtract, ALU.mult))
            v.done(nc.vector.tensor_scalar(se1[:, :], se1_in[:, :], 1.0 / D, None, ALU.mult))
            v.done(nc.vector.tensor_copy(se2[:, :, :], se2_in[:, :].unsqueeze(2).broadcast_to([SE + 1, NF, P])))
            dve.wait_ge(s_pra, 6)
            v.done(nc.vector.tensor_tensor(target[:, :], fields[:, 2, :], fields[:, 3, :], ALU.add))
            dve.wait_ge(s_pro, 6)
            v.done(nc.vector.tensor_scalar(u_neg[:, :], pM[:, 0:B], vec[:, R_AB1:R_AB1 + 1], -1.0,
                                           ALU.add, ALU.mult))
            dve.wait_ge(s_pro, 7)
            v.done(nc.vector.tensor_scalar(c_row[:, :], pT[:, 0:NT], -1.0, ab2[:, 0:1], ALU.mult, ALU.add))
            v.wait()

            def chunk(g, j, c):
                n = j * NC + c
                dve.wait_ge(s_st, CPG * g + n + 1)
                nc.vector.tensor_tensor(
                    p_t[:, :].rearrange("p (s b) -> p s b", b=P), s_t[:, :].rearrange("p (s b) -> p s b", b=P),
                    target[:, bass.ds(g * G + j * P, P)].unsqueeze(1).broadcast_to([P, CH, P]), ALU.mult).then_inc(s_pt, 1)
                dve.wait_ge(s_h, CPG * g + n + 1)
                dve.wait_ge(s_sc, CPG * g + n)
                nc.vector.tensor_tensor(
                    act_h[:, :].rearrange("p (s b) -> p s b", b=P), pH[:, 0:HC * P].rearrange("p (s b) -> p s b", b=P),
                    u_neg[:, bass.ds(g * G + j * P, P)].unsqueeze(1).broadcast_to([P, HC, P]), ALU.max).then_inc(s_ah, 1)

            def softmax(g, j):
                dve.wait_ge(s_sc, CPG * g + NC * (j + 1))
                t = 2 * g + j
                nc.vector.scalar_tensor_tensor(
                    out=logit[:, :], in0=pA[:, j * BANK:j * BANK + S], scalar=c_row[:, bass.ds(t, 1)],
                    in1=kept[:, bass.ds(t, 1), :].rearrange("p a s -> p (a s)"), op0=ALU.add, op1=ALU.mult)\
                    .then_inc(s_scf[j], 1)
                dve.wait_ge(s_scf[j], g + 1)
                v.done(nc.vector.tensor_tensor(logit[:, :], logit[:, :],
                                               masked[:, bass.ds(t, 1), :].rearrange("p a s -> p (a s)"), ALU.add))
                v.wait()
                v.done(nc.vector.tensor_reduce(top[:, 0:1], logit[:, :], AX_X, ALU.max))
                v.wait()
                nc.vector.tensor_scalar(top[:, 0:1], top[:, 0:1], -1.0, None, ALU.mult).then_inc(s_top, 1)
                dve.wait_ge(s_exp, t + 1)
                v.done(nc.vector.reciprocal(total[:, 0:1], total[:, 0:1]))
                v.wait()
                nc.vector.tensor_scalar(probs[:, :], exps[:, :], total[:, 0:1], None, ALU.mult).then_inc(s_prb, 1)
                dve.wait_ge(s_prb, t + 1)
                for s in range(2):
                    v.done(nc.vector.tensor_scalar(hist[:, s, :], seq[j][:, s, :], probs[:, s:s + 1], None, ALU.mult))
                for s in range(2, S):
                    v.wait(1)
                    v.done(nc.vector.scalar_tensor_tensor(
                        out=hist[:, s % 2, :], in0=seq[j][:, s, :], scalar=probs[:, s:s + 1],
                        in1=hist[:, s % 2, :], op0=ALU.mult, op1=ALU.add))
                v.wait()
                nc.vector.tensor_tensor(hist[:, 0, :], hist[:, 0, :], hist[:, 1, :], ALU.add).then_inc(s_hist[j], 1)

            def lo_part(to, of, hi):
                return nc.vector.tensor_tensor(to, of, hi, ALU.subtract)

            def assemble(g):
                dve.wait_ge(s_sq, g + 1)
                nc.vector.tensor_scalar(squeeze[0:SE, :], pM[0:SE, 128:128 + G], se_b1[:, 0:1], 0.0,
                                        ALU.add, ALU.max).then_inc(s_sqr, 1)
                dve.wait_ge(s_gr, g + 1)
                nc.vector.tensor_tensor(se[:, :, :], fields[:, :, bass.ds(g * G, G)], gate[:, :, :],
                                        ALU.mult).then_inc(s_se, 1)
                dve.wait_ge(s_dh, NF * g + 1)
                part = xd[:, bass.ds(g, 1), :, :, :].rearrange("p a h k n -> p (a h) k n")
                lo_part(part[:, 1, 0:NF, :], se[:, :, :], f32(part[:, 0, 0:NF, :])).then_inc(s_dl, 1)
                at = NF
                dve.wait_ge(s_se, g + 1)
                for i in range(NV + 1):
                    if i < NV:
                        dve.wait_ge(s_vid, g + 1)
                        if i >= 2:
                            dve.wait_ge(s_dl, NF * g + i)
                        nc.vector.tensor_tensor(
                            prod[:, i % 2, 0:(NV - i) * G].rearrange("p (k n) -> p k n", n=G),
                            pH[:, i * G:(i + 1) * G].unsqueeze(1).broadcast_to([P, NV - i, G]), se[:, i + 1:NF, :],
                            ALU.mult).then_inc(s_pr, 1)
                    if i:
                        w = NV - i + 1
                        dve.wait_ge(s_dh, NF * g + i + 1)
                        lo_part(part[:, 1, at:at + w, :], prod[:, (i - 1) % 2, 0:w * G].rearrange("p (k n) -> p k n", n=G),
                                f32(part[:, 0, at:at + w, :])).then_inc(s_dl, 1)
                        at += w

            with dve.Fori(0, NG) as g:
                v.enter(g, 2 * (3 + S))
                for j in range(2):
                    for c in range(NC):
                        chunk(g, j, c)
                    softmax(g, j)
                assemble(g)
                v.leave(NG)

            def split_w(j, n, width=KT * P):
                dve.wait_ge(s_wh, n + 1)
                dve.wait_ge(s_mm, n - 1)
                lo_part(w_lo[:, j, 0:width], w_raw[:, j, 0:width], f32(w_hi[:, j, 0:width])).then_inc(s_wl, 1)

            def by_group(x):
                return x.rearrange("p (g n) -> p g n", g=NG)

            def at_block(x, h, m):
                return x[:, :, h, bass.ds(m, 1), :].rearrange("p g a n -> p g (a n)")

            def cross(l, m, j, n):
                dve.wait_ge(s_mm, n + 1)
                dve.wait_ge(s_dn, n + 1)
                if l == 0:
                    steps = [dn[:, j, :]]
                else:
                    steps = [f32(at_block(xe, 0, m)), f32(at_block(xe, 1, m))]
                nc.vector.scalar_tensor_tensor(
                    out=xf[:, j, :], in0=pA[:, j * BANK:j * BANK + B], scalar=vec[:, bass.ds(m + l * KT, 1)],
                    in1=dn[:, j, :], op0=ALU.add, op1=ALU.mult).then_inc(s_dve, 1)
                v.n += 1
                for q, term in enumerate(steps):
                    v.wait()
                    ins = nc.vector.tensor_tensor(by_group(xf[:, j, :]), by_group(xf[:, j, :]),
                                                  by_group(term) if l == 0 else term, ALU.add)
                    if q < len(steps) - 1:
                        v.done(ins)
                    else:
                        ins.then_inc(s_xf[j], 1)

            def cross_lo(to, m, j, n):
                dve.wait_ge(s_xh, n + 1)
                lo_part(at_block(to, 1, m), by_group(xf[:, j, :]), f32(at_block(to, 0, m))).then_inc(s_xl, 1)

            for n in range(2):
                dve.wait_ge(s_wh, n + 1)
                lo_part(w_lo[:, n, :], w_raw[:, n, :], f32(w_hi[:, n, :])).then_inc(s_wl, 1)
            with dve.Fori(0, KT // 2) as i:
                v.enter(i, 2)
                for j in range(2):
                    cross(0, 2 * i + j, j, 2 * i + j)
                    split_w(j, 2 * i + j + 2)
                    cross_lo(xe, 2 * i + j, j, 2 * i + j)
                v.leave(KT // 2)
            cross(0, KT - 1, 0, KT - 1)
            cross_lo(xe, KT - 1, 0, KT - 1)
            split_w(0, KT + 1)
            cross(1, 0, 1, KT)
            split_w(1, KT + 2)
            cross_lo(xd, 0, 1, KT)
            with dve.Fori(0, KT // 2 - 1) as i:
                v.enter(i, 4)
                for j in range(2):
                    cross(1, 2 * i + 1 + j, j, 2 * i + j + KT + 1)
                    split_w(j, 2 * i + j + KT + 3)
                    cross_lo(xd, 2 * i + 1 + j, j, 2 * i + j + KT + 1)
                v.leave(KT // 2 - 1)
            for n in range(NL * KT - 2, ITEMS - 2):
                if n < NL * KT:
                    cross(1, n - KT, n % 2, n)
                    cross_lo(xd, n - KT, n % 2, n)
                split_w(n % 2, n + 2, W1K * N1)

            def norm(of, to, n, roots):
                for t in range(NT):
                    v.done(nc.vector.bn_stats(stats[:, t, :], of(t)))
                v.wait()
                for t in range(NT):
                    v.done(nc.vector.bn_aggr(moments[:, t, :], stats[:, t, :]))
                v.wait()
                nc.vector.tensor_scalar(spread[:, :], moments[:, :, 1], EPS, None, ALU.add).then_inc(s_hat, 1)
                dve.wait_ge(s_sqrt, roots)
                v.done(nc.vector.reciprocal(spread[:, :], spread[:, :]))
                v.wait()
                for t in range(NT):
                    ins = nc.vector.tensor_scalar(to[:, t, :], of(t), moments[:, t, 0:1], spread[:, t:t + 1],
                                                  ALU.subtract, ALU.mult)
                ins.then_inc(s_hat, 1)

            dve.wait_ge(s_w1, 1)
            norm(lambda t: pT[:, t * BANK:(t + 1) * BANK] if t < 3 else pH[:, 0:BANK], hat1, N1, 2)
            dve.wait_ge(s_w2, 1)
            norm(lambda t: pA[:, t * N2:(t + 1) * N2], hat2, N2, 3)

        @block.tensor
        def _(pe):
            mm, tr = nc.tensor.matmul, nc.tensor.transpose
            pe.wait_ge(s_small, 16 * len(SMALL))
            tr(pM[:, 0:NR], vec_rows[:, :], ident[0:NR, 0:NR])
            for t in range(NT):
                ins = tr(pT[:, t * P:(t + 1) * P], emb[:, t, :], ident[:, :])
            ins.then_inc(s_pro, 1)
            pe.wait_ge(s_dve, 6)
            for j in range(2):
                ins = mm(pT[:, (1 + j) * BANK:(1 + j) * BANK + B], cate[:, :], one_hot[:, j, :], start=True, stop=True)
            ins.then_inc(s_pro, 1)
            pe.wait_ge(s_pra, 2)
            for t in range(NT):
                mm(pH[:, t * D:(t + 1) * D], ones[0:1, :], mm_b[0:1, :], start=True, stop=False)
                ins = mm(pH[:, t * D:(t + 1) * D], emb_t[:, t, :], mm_w[:, :], start=False, stop=True)
            ins.then_inc(s_pro, 1)
            pe.wait_ge(s_idr, 16 * NT)
            for t in range(NT):
                ins = tr(pT[:, t * P:(t + 1) * P], id_rows[:, t, :], ident[:, :])
            ins.then_inc(s_pro, 1)
            pe.wait_ge(s_dve, 12 + 3 * NT)
            pe.wait_ge(s_pra, 4)
            for t in range(NT):
                ins = tr(pT[:, BANK + t * P:BANK + (t + 1) * P], img_hat[:, t, :], ident[:, :])
            ins.then_inc(s_pro, 1)
            pe.wait_ge(s_dve, 15 + 3 * NT)
            mm(pM[:, 0:B], w_u[:, :, :].rearrange("p h n -> p (h n)"), target[:, :], start=True, stop=True)\
                .then_inc(s_pro, 1)
            pe.wait_ge(s_dve, 16 + 3 * NT)
            for t in range(NT):
                ins = mm(pT[:, t:t + 1], u_neg[:, t * P:(t + 1) * P], vec[:, R_AW2:R_AW2 + 1], start=True, stop=True)
            ins.then_inc(s_pro, 1)
            pe.wait_ge(s_dve, 17 + 3 * NT)

            with pe.Fori(0, NG) as g:
                for j in range(2):
                    for c in range(NC):
                        n = j * NC + c
                        pe.wait_ge(s_rows[n], 16 * CH * (g + 1))
                        pe.wait_ge(s_st, CPG * g + n)
                        if n == 0:
                            pe.wait_ge(s_gr, g)
                        for s in range(CH):
                            ins = tr(pT[:, s * P:(s + 1) * P], seq[j][:, c * CH + s, :], ident[:, :])
                        ins.then_inc(s_tr, 1)
                        pe.wait_ge(s_st, CPG * g + n + 1)
                        pe.wait_ge(s_pt, CPG * g + n + 1)
                        pe.wait_ge(s_ah, CPG * g + n)
                        if n == 0:
                            pe.wait_ge(s_pr, NV * g)
                        for s0, ns in ((0, 4), (4, HC - 4)):
                            for w, x in ((w_s, s_t), (w_p, p_t)):
                                for h in range(2):
                                    at = (h * HC + s0) * P
                                    ins = mm(pH[h * HID:(h + 1) * HID, s0 * P:(s0 + ns) * P], w[:, :],
                                             x[:, at:at + ns * P], start=(w is w_s), stop=(w is w_p))
                        ins.then_inc(s_h, 1)
                        pe.wait_ge(s_ah, CPG * g + n + 1)
                        if c == 0:
                            pe.wait_ge(s_scf[j], g)
                        for s in range(HC):
                            o = j * BANK + c * CH + s
                            ins = mm(pA[:, o:o + HC + 1:HC], act_h[:, s * P:(s + 1) * P], vec[:, R_AW2:R_AW2 + 2],
                                     start=True, stop=True)
                        ins.then_inc(s_sc, 1)
                    pe.wait_ge(s_hist[j], g + 1)
                    pe.wait_ge(s_hc, 2 * g + j)
                    pe.wait_ge(s_sqr, g)
                    tr(pM[:, 384:384 + P], hist[:, 0, :], ident[:, :]).then_inc(s_ht, 1)
                pe.wait_ge(s_hc, 2 * g + 2)
                for f in range(NF):
                    ins = mm(pM[0:SE, 128:128 + G], se1[:, f * SE:(f + 1) * SE], fields[:, f, bass.ds(g * G, G)],
                             start=(f == 0), stop=(f == NF - 1))
                ins.then_inc(s_sq, 1)
                pe.wait_ge(s_sqr, g + 1)
                for f in range(NF):
                    ins = mm(pT[:, f * G:(f + 1) * G], se2[:, f, :], squeeze[:, :], start=True, stop=True)
                ins.then_inc(s_ga, 1)
                pe.wait_ge(s_se, g + 1)
                for f in range(NV):
                    ins = mm(pH[:, f * G:(f + 1) * G], bil_w[:, f, :], se[:, f, :], start=True, stop=True)
                ins.then_inc(s_vid, 1)

            def cross_block(j, x, n, last_lo=None):
                pe.wait_ge(s_wl, n + 1)
                acc = pA[:, j * BANK:j * BANK + B].rearrange("p (g n) -> p g n", g=NG)
                for k in range(KT):
                    if last_lo and k == KT - 1:
                        pe.wait_ge(s_xl, last_lo)
                    hi, lo = w_hi[:, j, k * P:(k + 1) * P], w_lo[:, j, k * P:(k + 1) * P]
                    mm(acc, hi, x[:, :, 0, k, :], start=(k == 0), stop=False)
                    mm(acc, hi, x[:, :, 1, k, :], start=False, stop=False)
                    ins = mm(acc, lo, x[:, :, 0, k, :], start=False, stop=(k == KT - 1))
                ins.then_inc(s_mm, 1)

            pe.wait_ge(s_dl, NF * NG)
            with pe.Fori(0, KT // 2) as i:
                for j in range(2):
                    pe.wait_ge(s_xf[j], i)
                    cross_block(j, xd, 2 * i + j)
            pe.wait_ge(s_xf[0], KT // 2)
            cross_block(0, xd, KT - 1)
            pe.wait_ge(s_xf[1], KT // 2)
            pe.wait_ge(s_xl, KT - 1)
            cross_block(1, xe, KT, last_lo=KT)
            with pe.Fori(0, KT // 2) as i:
                for j in range(2):
                    pe.wait_ge(s_xf[j], i + (KT + 1) // 2)
                    cross_block(j, xe, KT + 1 + 2 * i + j)

            def bank(t):
                return pT[:, t * BANK:t * BANK + N1] if t < 3 else pH[:, 0:N1]

            for t in range(NT):
                mm(bank(t), ones[0:1, :], b1[0:1, :], start=True, stop=False)
            for q in range(NW1):
                n = NL * KT + q
                pe.wait_ge(s_wl, n + 1)
                for k in range(W1K):
                    if q == NW1 - 1 and k == W1K - 1:
                        pe.wait_ge(s_xl, NL * KT)
                    elif k == 0:
                        pe.wait_ge(s_xl, NL * KT - KT + min(KT, (q + 1) * W1K) - (q == NW1 - 1))
                    hi = w_hi[:, n % 2, k * N1:(k + 1) * N1]
                    lo = w_lo[:, n % 2, k * N1:(k + 1) * N1]
                    kk = q * W1K + k
                    for t in range(NT):
                        x_hi = xd[:, t // 2, 0, kk, (t % 2) * P:(t % 2) * P + P]
                        x_lo = xd[:, t // 2, 1, kk, (t % 2) * P:(t % 2) * P + P]
                        mm(bank(t), x_hi, hi, start=False, stop=False)
                        mm(bank(t), x_hi, lo, start=False, stop=False)
                        ins = mm(bank(t), x_lo, hi, start=False, stop=(kk == KT - 1))
                ins.then_inc(s_mm if q < NW1 - 1 else s_w1, 1)

            pe.wait_ge(s_hat, 2)
            for c in range(K1):
                if c >= 2:
                    pe.wait_ge(s_ge, c - 1)
                to = pM if c % 2 else pH
                o = 0 if c % 2 else BANK
                for t in range(NT):
                    ins = tr(to[:, o + t * P:o + (t + 1) * P], hat1[:, t, c * P:(c + 1) * P], ident[:, :])
                ins.then_inc(s_mt, 1)
            for j in range(2):
                pe.wait_ge(s_xf[j], NL * KT // 2)
            pe.wait_ge(s_ge, K1)
            for t in range(NT):
                mm(pA[:, t * N2:(t + 1) * N2], ones[0:1, :], b2[0:1, :], start=True, stop=False)
                for c in range(K1):
                    ins = mm(pA[:, t * N2:(t + 1) * N2], h1_t[:, c, t * P:(t + 1) * P], w2[:, c, :],
                             start=False, stop=(c == K1 - 1))
            ins.then_inc(s_w2, 1)
            pe.wait_ge(s_hat, 4)
            for c in range(K2):
                for t in range(NT):
                    ins = tr(pT[:, c * BANK + t * P:c * BANK + (t + 1) * P], hat2[:, t, c * P:(c + 1) * P], ident[:, :])
                ins.then_inc(s_mt, 1)
            pe.wait_ge(s_ge, K1 + K2)
            for c in range(K2):
                ins = mm(pH[0:1, 0:B], vec[:, R_W3 + c:R_W3 + c + 1], h2_t[:, c, :], start=(c == 0), stop=(c == K2 - 1))
            ins.then_inc(s_w3, 1)


def kernel(**inputs):
    import numpy as np
    import concourse.bacc as bacc
    from concourse.bass_utils import run_bass_kernel_spmd

    nc = bacc.Bacc("TRN2", target_bir_lowering=False, num_devices=1)
    arrays, aps = {}, {}
    for name in INS:
        arr = np.ascontiguousarray(inputs[name])
        arrays[f"in_{name}"] = arr
        aps[name] = nc.dram_tensor(f"in_{name}", arr.shape, mybir.dt.from_np(arr.dtype), kind="ExternalInput").ap()
    consts = {"ident": np.eye(P, dtype=np.float32),
              "iota": np.arange(inputs['L0_rec_cate_table'].shape[0], dtype=np.float32).reshape(-1, 1)}
    for name, arr in consts.items():
        arrays[f"in_{name}"] = arr
        aps[name] = nc.dram_tensor(f"in_{name}", arr.shape, F32, kind="ExternalInput").ap()
    B = inputs['r_item_id'].shape[0]
    out = nc.dram_tensor("out_y", (B,), F32, kind="ExternalOutput").ap()
    build(nc, aps, aps["ident"], aps["iota"], out)
    r = run_bass_kernel_spmd(nc, [arrays], core_ids=[0])
    return r.results[0]["out_y"]
```

```python
from contextlib import ExitStack

import concourse.bass as bass
from concourse import mybir

F32 = mybir.dt.float32
F32R = mybir.dt.float32r
I32 = mybir.dt.int32
ALU = mybir.AluOpType
ACT = mybir.ActivationFunctionType
AX_X = mybir.AxisListType.X

P = 128
BANK = 512
EPS = 1e-5
MASKED = -1000000000.0
LEAST = -3.0e38

INS = ['r_item_emb_d128', 'r_item_id', 'r_likes_level', 'r_views_level', 'r_item_seq',
       'L0_rec_item_table', 'L0_rec_cate_table', 'L0_rec_mm_w', 'L0_rec_mm_b', 'L0_rec_mm_ln_g',
       'L0_rec_mm_ln_b', 'L0_rec_aw1', 'L0_rec_ab1', 'L0_rec_aw2', 'L0_rec_ab2', 'L0_rec_se_w1',
       'L0_rec_se_b1', 'L0_rec_se_w2', 'L0_rec_se_b2', 'L0_rec_bil_W', 'L0_rec_cross_K',
       'L0_rec_cross_bias', 'L0_rec_w1', 'L0_rec_b1', 'L0_rec_ln1g', 'L0_rec_ln1b', 'L0_rec_w2',
       'L0_rec_b2', 'L0_rec_ln2g', 'L0_rec_ln2b', 'L0_rec_w3', 'L0_rec_b3']


class Steps:

    def __init__(self, eng, sem):
        self.eng, self.sem, self.n, self.i, self.per = eng, sem, 0, None, 0

    def done(self, instruction):
        instruction.then_inc(self.sem, 1)
        self.n += 1

    def wait(self, behind=0):
        n = self.n - behind
        self.eng.wait_ge(self.sem, n if self.i is None else self.i * self.per + n)

    def enter(self, i, per):
        self.i, self.per, self.start = i, per, self.n

    def leave(self, trips):
        assert self.n - self.start == self.per, (self.n - self.start, self.per)
        self.n = self.start + self.per * trips
        self.i = None


def build(nc, a, ident_in, iota_in, out):
    B, S = a['r_item_seq'].shape
    D = a['L0_rec_item_table'].shape[1]
    LV = a['L0_rec_cate_table'].shape[0]
    HID = a['L0_rec_aw1'].shape[1]
    NF, SE = a['L0_rec_se_w1'].shape
    NL, TD, _ = a['L0_rec_cross_K'].shape
    N1 = a['L0_rec_w1'].shape[1]
    N2 = a['L0_rec_w2'].shape[1]
    NT = B // P
    NG = NT // 2
    G = 2 * P
    CH = 5
    CPG = S // CH
    RING = CPG // 2
    CW = 2 * CH
    HALF_C = CH * P
    KT = TD // P
    NV = NF - 1
    W1K = 3
    NW1 = KT // W1K
    K1 = N1 // P
    K2 = N2 // P
    assert D == P and 2 * HID == P and B == 4 * P and S % 10 == 0 and NL == 2
    assert KT % 2 == 1 and NW1 * W1K == KT and KT >= CPG + 5
    L0B, L1, MLP0 = KT, 2 * KT, 3 * KT
    ITEMS = MLP0 + NW1

    R_CB, R_G1 = 0, NL * KT
    R_B1 = R_G1 + K1
    R_G2 = R_B1 + K1
    R_B2 = R_G2 + K2
    R_MG = R_B2 + K2
    R_MB = R_MG + 1
    R_W3 = R_MB + 1
    R_AB1 = R_W3 + K2
    R_AW2 = R_AB1 + 1
    NR = R_AW2 + 2

    ctx = ExitStack()
    with ctx:
        def sb(name, shape, dt=F32, at=ctx):
            return at.enter_context(nc.sbuf_tensor(name, shape, dt))

        def ps(name, shape):
            return ctx.enter_context(nc.psum_tensor(name, shape, F32))

        def sem(name):
            return ctx.enter_context(nc.semaphore(name))

        PART = 2 * KT * G
        with ExitStack() as early:
            used = [0]

            def eb(name, shape, dt=F32):
                n = 1
                for x in shape[1:]:
                    n *= x
                used[0] += n
                return sb(name, shape, dt, early)

            def fill(name, parts):
                eb(name, [P, parts * PART - used[0]])

            emb = eb("emb", [P, NT, D])
            emb_t = eb("emb_t", [P, NT, P])
            img_hat = eb("img_hat", [P, NT, D])
            id_rows = eb("id_rows", [P, NT, D])
            levels_i = eb("levels_i", [LV, 2, B], I32)
            levels_f = eb("levels_f", [LV, 2, B])
            one_hot = eb("one_hot", [LV, 2, B])
            vec_rows = eb("vec_rows", [NR, P])
            aw1 = eb("aw1", [P, 4, HID])
            mm_w = eb("mm_w", [P, D])
            cate = eb("cate", [LV, D])
            mm_b = eb("mm_b", [1, D])
            idx = eb("idx", [P, NT, S], I32)
            masked = eb("masked", [P, NG * CPG, CW])
            fill("fill_xd0", 1)
            seq = eb("seq", [P, RING, 2, CH, D])
            s_t = eb("s_t", [P, CW * P])
            with ExitStack() as mlp:
                hat1 = sb("hat1", [P, NT, N1], F32, mlp)
                h1_t = sb("h1_t", [P, K1, B], F32, mlp)
                hat2 = sb("hat2", [P, NT, N2], F32, mlp)
                h2_t = sb("h2_t", [P, K2, B], F32, mlp)
            fill("fill_xe0", 3)
            p_t = eb("p_t", [P, CW * P])
            se = eb("se", [P, NF, G])
            gate = eb("gate", [P, NF, G])
            prod = eb("prod", [P, 2, NV * G])
        xd = sb("xd", [P, NG, 2, KT, G], F32R)
        xe = sb("xe", [P, NG, 2, KT, G], F32R)
        target = sb("target", [P, B])
        u_neg = sb("u_neg", [P, NG * P])
        act_h = sb("act_h", [P, HALF_C])
        dn = sb("dn", [P, B])
        xf = sb("xf", [P, 2, B])
        w_raw = sb("w_raw", [P, 2, KT * P])
        w_hi = sb("w_hi", [P, 2, KT * P], F32R)
        w_lo = sb("w_lo", [P, 2, KT * P], F32R)
        fields = sb("fields", [P, NF, B])
        ident = sb("ident", [P, P])
        iota = sb("iota", [LV, 1])
        vec = sb("vec", [P, NR])
        w_u = sb("w_u", [P, HID])
        w_s = sb("w_s", [P, HID])
        w_p = sb("w_p", [P, HID])
        bil_w = sb("bil_w", [P, NV, D])
        w2 = sb("w2", [P, K1, N2])
        ones = sb("ones", [1, P])
        b1 = sb("b1", [1, N1])
        b2 = sb("b2", [1, N2])
        ab2 = sb("ab2", [P, 1])
        b3 = sb("b3", [1, 1])
        se1_in = sb("se1_in", [P, NF * SE])
        se1 = sb("se1", [P, NF * SE])
        se_b1 = sb("se_b1", [SE, 1])
        se2_in = sb("se2_in", [SE + 1, NF])
        se2 = sb("se2", [SE + 1, NF, P])
        squeeze = sb("squeeze", [SE + 1, G])
        idx_c = sb("idx_c", [P, NG * CPG, CW], I32)
        idx_g = sb("idx_g", [P, RING, CW], I32)
        ids = sb("ids", [P, NT], I32)
        kept = sb("kept", [P, NG * CPG, CW])
        shift = sb("shift", [P, NG * CPG, CW])
        c_row = sb("c_row", [P, NT])
        logit = sb("logit", [P, RING, 2, CH + 1])
        diff = sb("diff", [P, 2, CH + 1])
        exps = sb("exps", [P, 2, CH + 1])
        total = sb("total", [P, 2])
        part_sum = sb("part_sum", [P, 2])
        hist = sb("hist", [P, 2, D])
        stats = sb("stats", [P, NT, 6])
        moments = sb("moments", [P, NT, 2])
        spread = sb("spread", [P, NT])
        minus_half = sb("minus_half", [P, 1])
        y = sb("y", [1, B])

        pT = ps("pT", [P, 3 * BANK])
        pH = ps("pH", [P, 2 * BANK])
        pM = ps("pM", [P, BANK])
        pA = ps("pA", [P, 2 * BANK])

        s_idx = sem("idx_loaded")
        s_idc = sem("idx_by_chunk")
        s_small = sem("small_loaded")
        s_late = sem("late_loaded")
        s_idr = sem("id_rows_landed")
        s_idxg = sem("idx_chunk_ready")
        s_seen = sem("idx_chunk_seen")
        s_rows = [sem(f"rows_landed{r}") for r in range(RING)]
        s_slot = sem("ring_slots_free")
        s_raw = [sem(f"w_raw_landed{j}") for j in range(2)]
        s_out = sem("out_stored")
        s_vz = sem("vec_rows_zeroed")
        s_pro = sem("prologue_pe")
        s_pra = sem("prologue_act")
        s_dve = sem("dve_step")
        s_sqrt = sem("roots_taken")
        s_tr = sem("chunk_transposed")
        s_st = sem("s_t_ready")
        s_h = sem("hidden_done")
        s_ah = sem("act_h_ready")
        s_sc = sem("scores_done")
        s_scr = sem("scores_read")
        s_pt = sem("p_t_ready")
        s_dif = sem("diff_ready")
        s_exp = sem("exps_ready")
        s_hist = sem("hist_ready")
        s_ht = sem("hist_transposed")
        s_hc = sem("hist_copied")
        s_sq = sem("squeeze_summed")
        s_sqr = sem("squeeze_ready")
        s_ga = sem("gate_summed")
        s_gr = sem("gate_ready")
        s_se = sem("se_ready")
        s_vid = sem("vids_done")
        s_pr = sem("prod_ready")
        s_dh = sem("xd_hi_ready")
        s_dl = sem("xd_lo_ready")
        s_wh = sem("w_hi_ready")
        s_wl = sem("w_lo_ready")
        s_mm = sem("block_done")
        s_xf = [sem(f"xf_ready{j}") for j in range(2)]
        s_xh = sem("x_hi_ready")
        s_xl = sem("x_lo_ready")
        s_w1 = sem("w1_done")
        s_var = sem("variances_ready")
        s_pow = sem("spreads_ready")
        s_hat = sem("hats_ready")
        s_mt = sem("mlp_transposed")
        s_ge = sem("gelu_done")
        s_w2 = sem("w2_done")
        s_w3 = sem("w3_done")
        s_y = sem("y_ready")

        def f32(ap):
            return ap.bitcast(F32)

        K = a['L0_rec_cross_K'].rearrange("l (k p) n -> l p k n", p=P)
        W1 = a['L0_rec_w1'].rearrange("(k p) n -> p k n", p=P)
        W2 = a['L0_rec_w2'].rearrange("(k p) n -> p k n", p=P)

        def row(name, n=1):
            return a[name].rearrange("(a n) -> a n", a=n)

        SMALL, LATE = [], []

        def groups(n_first):
            return slice(0, 1) if n_first < L0B else slice(1, 2) if n_first < L1 else slice(0, 2)

        def at_block(x, h, m, gs):
            return x[:, gs, h, bass.ds(m, 1), :].rearrange("p g a n -> p g (a n)")

        def by_group(x, gs):
            n = gs.stop - gs.start
            return x[:, 0:n * G].rearrange("p (g n) -> p g n", g=n)

        def first_acc(t):
            return pT[:, t * BANK:t * BANK + N1] if t < 3 else pH[:, 0:N1]

        def second_acc(t):
            return pA[:, t * BANK:t * BANK + N2] if t < 2 else pT[:, (t - 2) * BANK:(t - 2) * BANK + N2]

        PRO = {}

        block = ctx.enter_context(nc.Block())

        @block.sync
        def _(sp):
            sp.dma_start(idx[:, :, :], a['r_item_seq'].rearrange("(t p) s -> p t s", p=P)).then_inc(s_idx, 16)
            sp.dma_start(ids[:, :], a["r_item_id"].rearrange("(t p) -> p t", p=P),
                         allow_slow_non_contiguous=True).then_inc(s_idx, 16)

            def small(to, of):
                sp.dma_start(to, of).then_inc(s_small, 16)
                SMALL.append(1)

            def late(to, of):
                sp.dma_start(to, of).then_inc(s_late, 16)
                LATE.append(1)

            small(emb[:, :, :], a['r_item_emb_d128'].rearrange("(t p) d -> p t d", p=P))
            small(ident[:, :], ident_in)
            small(mm_w[:, :], a['L0_rec_mm_w'])
            small(mm_b[:, :], row('L0_rec_mm_b'))
            small(iota[:, :], iota_in)
            small(cate[:, :], a['L0_rec_cate_table'])
            for j, name in enumerate(('r_likes_level', 'r_views_level')):
                small(levels_i[:, j, :], row(name).broadcast_to([LV, B]))
            small(aw1[:, :, :], a['L0_rec_aw1'].rearrange("(q p) n -> p q n", p=P))
            sp.wait_ge(s_vz, 1)
            small(vec_rows[R_CB:R_G1, :], a['L0_rec_cross_bias'].rearrange("l (m p) -> (l m) p", p=P))
            small(vec_rows[R_G1:R_B1, :], row('L0_rec_ln1g', K1))
            small(vec_rows[R_B1:R_G2, :], row('L0_rec_ln1b', K1))
            small(vec_rows[R_G2:R_B2, :], row('L0_rec_ln2g', K2))
            small(vec_rows[R_B2:R_MG, :], row('L0_rec_ln2b', K2))
            small(vec_rows[R_MG:R_MB, :], row('L0_rec_mm_ln_g'))
            small(vec_rows[R_MB:R_W3, :], row('L0_rec_mm_ln_b'))
            small(vec_rows[R_W3:R_AB1, :], a['L0_rec_w3'].rearrange("(c p) a -> c (p a)", p=P))
            for h in range(2):
                small(vec_rows[R_AB1:R_AB1 + 1, h * HID:(h + 1) * HID], row('L0_rec_ab1'))
                small(vec_rows[R_AW2 + h:R_AW2 + h + 1, h * HID:(h + 1) * HID],
                      a['L0_rec_aw2'].rearrange("p a -> a p"))
            small(ab2[:, :], row('L0_rec_ab2').broadcast_to([P, 1]))
            late(se1_in[:, :], a['L0_rec_se_w1'].rearrange("(a f) i -> a (f i)", a=1).broadcast_to([P, NF * SE]))
            late(se_b1[:, :], a['L0_rec_se_b1'].rearrange("(p a) -> p a", a=1))
            late(se2_in[0:SE, :], a['L0_rec_se_w2'])
            late(se2_in[SE:SE + 1, :], row('L0_rec_se_b2'))
            late(bil_w[:, :, :], a['L0_rec_bil_W'].rearrange("f d e -> d f e"))
            late(b1[:, :], row('L0_rec_b1'))
            late(b2[:, :], row('L0_rec_b2'))
            late(b3[:, :], row('L0_rec_b3'))
            late(w2[:, :, :], W2)

            def load_block(l, m, n, j):
                sp.wait_ge(s_wl, n - 1)
                sp.dma_start(w_raw[:, j, :].rearrange("p (k n) -> p k n", k=KT),
                             K[l, :, :, bass.ds(m * P, P)]).then_inc(s_raw[j], 16)

            for j in range(2):
                sp.dma_start(w_raw[:, j, :].rearrange("p (k n) -> p k n", k=KT),
                             K[0, :, :, j * P:(j + 1) * P]).then_inc(s_raw[j], 16)
            with sp.Fori(0, (KT - 3) // 2) as i:
                for j in range(2):
                    load_block(0, 2 * i + 2 + j, 2 * i + 2 + j, j)
            load_block(0, KT - 1, KT - 1, 0)
            load_block(0, 0, L0B, 1)
            with sp.Fori(0, KT // 2) as i:
                for j in range(2):
                    load_block(0, 2 * i + 1 + j, 2 * i + 1 + j + L0B, j)
            with sp.Fori(0, KT // 2) as i:
                for j in range(2):
                    load_block(1, 2 * i + j, 2 * i + j + L1, j)
            load_block(1, KT - 1, MLP0 - 1, 0)
            for q in range(NW1):
                n = MLP0 + q
                sp.wait_ge(s_wl, n - 1)
                sp.dma_start(w_raw[:, n % 2, 0:W1K * N1].rearrange("p (k n) -> p k n", k=W1K),
                             W1[:, q * W1K:(q + 1) * W1K, :]).then_inc(s_raw[n % 2], 16)
            sp.wait_ge(s_y, 1)
            sp.dma_start(out.rearrange("(a n) -> a n", a=1), y[:, :]).then_inc(s_out, 16)
            sp.wait_ge(s_out, 16)

        @block.gpsimd
        def _(pool):
            nc.gpsimd.memset(vec_rows[:, :], 0.0).then_inc(s_vz, 1)
            nc.gpsimd.memset(minus_half[:, :], -0.5).then_inc(s_vz, 1)
            pool.wait_ge(s_idx, 32)
            table = a['L0_rec_item_table']
            for t in range(NT):
                nc.gpsimd.indirect_dma_start(
                    id_rows[:, t, :], None, table,
                    bass.IndirectOffsetOnAxis(ap=ids[:, t:t + 1], axis=0)).then_inc(s_idr, 16)
            pool.wait_ge(s_idc, NG)
            with pool.Fori(0, NG * CPG // RING) as i:
                for r in range(RING):
                    pool.wait_ge(s_slot, i * RING + r + 1)
                    nc.gpsimd.tensor_copy(idx_g[:, r, :],
                                          idx_c[:, bass.ds(i * RING + r, 1), :].rearrange("p a s -> p (a s)"))\
                        .then_inc(s_idxg, 1)
                    pool.wait_ge(s_idxg, i * RING + r + 1)
                    pool.sem_inc(s_seen, 1)
                    for q in range(CW):
                        nc.gpsimd.indirect_dma_start(
                            seq[:, r, q // CH, q % CH, :], None, table,
                            bass.IndirectOffsetOnAxis(ap=idx_g[:, r, q:q + 1], axis=0)).then_inc(s_rows[r], 16)

            pool.wait_ge(s_vz, 2)
            for n in range(NT + 1):
                pool.wait_ge(s_var, n + 1)
                cols = slice(n, n + 1) if n < NT else slice(0, NT)
                w = cols.stop - cols.start
                nc.gpsimd.tensor_tensor(spread[:, cols], spread[:, cols],
                                        minus_half[:, :].broadcast_to([P, w]), ALU.pow).then_inc(s_pow, 1)

        @block.scalar
        def _(act):
            act.sem_inc(s_st, 1)
            act.wait_ge(s_pro, 1)
            nc.scalar.copy(emb_t[:, :, :], pT[:, 0:B]).then_inc(s_pra, 1)
            act.wait_ge(s_pro, 2)
            nc.scalar.copy(vec[:, :], pM[:, 0:NR]).then_inc(s_pra, 1)
            for j in range(2):
                nc.scalar.copy(fields[:, j, :], pT[:, (1 + j) * BANK:(1 + j) * BANK + B]).then_inc(s_pra, 1)
            act.wait_ge(s_pro, 4)
            nc.scalar.copy(fields[:, 2, :], pT[:, 0:B]).then_inc(s_pra, 1)
            act.wait_ge(s_sqrt, 1)
            nc.scalar.activation(spread[:, :], spread[:, :], ACT.Sqrt).then_inc(s_sqrt, 1)
            act.wait_ge(s_pro, 5)
            act.wait_ge(s_pra, 2)
            nc.scalar.activation(fields[:, 3, :], pT[:, BANK:BANK + B], ACT.Gelu,
                                 scale=vec[:, R_MG:R_MG + 1], bias=vec[:, R_MB:R_MB + 1]).then_inc(s_pra, 1)

            def chunk_copy(n):
                act.wait_ge(s_tr, n + 1)
                act.wait_ge(s_h, n + 1)
                nc.scalar.copy(s_t[:, :], pT[:, 0:CW * P]).then_inc(s_st, 1)

            def chunk_exp(n):
                act.wait_ge(s_dif, n + 1)
                nc.scalar.activation(exps[:, :, :], diff[:, :, :], ACT.Exp).then_inc(s_exp, 1)

            def split_w(j, n, turn, width=KT * P):
                act.wait_ge(s_raw[j], 16 * turn)
                if not isinstance(n, int) or n >= 2:
                    act.wait_ge(s_mm, n - 1)
                nc.scalar.copy(w_hi[:, j, 0:width], w_raw[:, j, 0:width]).then_inc(s_wh, 1)

            def split_x(to, m, j, turn, gs):
                act.wait_ge(s_xf[j], turn + 1)
                nc.scalar.copy(at_block(to, 0, m, gs), by_group(xf[:, j, :], gs)).then_inc(s_xh, 1)

            def after(n):
                split_w(n % 2, n + 2, (n + 2) // 2 + 1)
                split_x(xe, n, n % 2, n // 2, groups(n))

            with act.Fori(0, CPG // RING) as i:
                for r in range(RING):
                    chunk_copy(i * RING + r)
                    chunk_exp(i * RING + r)

            def hist_out(g):
                act.wait_ge(s_ht, g + 1)
                nc.scalar.copy(fields[:, NF - 1, g * G:(g + 1) * G], pM[:, 0:G]).then_inc(s_hc, 1)

            def gates(g):
                act.wait_ge(s_ga, g + 1)
                nc.scalar.activation(gate[:, :, :], pT[:, 0:NF * G].rearrange("p (f n) -> p f n", f=NF),
                                     ACT.Sigmoid).then_inc(s_gr, 1)

            def fields_hi(g):
                act.wait_ge(s_se, g + 1)
                nc.scalar.copy(xd[:, g, 0, 0:NF, :], se[:, :, :]).then_inc(s_dh, 1)

            def products_hi(g):
                at = NF
                for i in range(NV):
                    act.wait_ge(s_pr, NV * g + i + 1)
                    nc.scalar.copy(xd[:, g, 0, at:at + NV - i, :],
                                   prod[:, i % 2, 0:(NV - i) * G].rearrange("p (k n) -> p k n", n=G))\
                        .then_inc(s_dh, 1)
                    at += NV - i

            for n in range(2):
                split_w(n, n, 1)
            hist_out(0)
            gates(0)
            fields_hi(0)
            products_hi(0)
            for c in range(CPG):
                chunk_copy(CPG + c)
                if c:
                    after(c - 1)
                chunk_exp(CPG + c)
            after(CPG - 1)
            after(CPG)
            hist_out(1)
            after(CPG + 1)
            gates(1)
            after(CPG + 2)
            fields_hi(1)
            after(CPG + 3)
            products_hi(1)
            after(CPG + 4)
            gs = groups(L0B)
            split_w(1, L0B + 2, (L0B + 2) // 2 + 1)
            split_x(xe, 0, 1, L0B // 2, gs)
            with act.Fori(0, KT // 2) as i:
                for j in range(2):
                    split_w(j, 2 * i + j + L0B + 3, i + (L0B + 3) // 2 + 1)
                    split_x(xe, 2 * i + j + 1, j, i + (L0B + 1) // 2, gs)
            gs = groups(L1)
            with act.Fori(0, KT // 2 - 1) as i:
                for j in range(2):
                    split_w(j, 2 * i + j + L1 + 2, i + L1 // 2 + 2)
                    split_x(xd, 2 * i + j, j, i + L1 // 2, gs)
            for n in range(MLP0 - 3, ITEMS - 2):
                split_w(n % 2, n + 2, (n + 2) // 2 + 1, KT * P if n + 2 < MLP0 else W1K * N1)
                if n < MLP0:
                    split_x(xd, n - L1, n % 2, n // 2, gs)

            for c in range(K1):
                act.wait_ge(s_mt, c + 1)
                nc.scalar.activation(h1_t[:, c, :], pM[:, :] if c % 2 else pH[:, BANK:2 * BANK], ACT.Gelu,
                                     scale=vec[:, R_G1 + c:R_G1 + c + 1],
                                     bias=vec[:, R_B1 + c:R_B1 + c + 1]).then_inc(s_ge, 1)
            for c in range(K2):
                act.wait_ge(s_mt, K1 + c + 1)
                nc.scalar.activation(h2_t[:, c, :], pM[:, :] if c % 2 else pH[:, BANK:2 * BANK], ACT.Gelu,
                                     scale=vec[:, R_G2 + c:R_G2 + c + 1],
                                     bias=vec[:, R_B2 + c:R_B2 + c + 1]).then_inc(s_ge, 1)
            act.wait_ge(s_w3, 1)
            nc.scalar.activation(y[:, :], pH[0:1, 0:B], ACT.Sigmoid, bias=b3[0:1, 0:1]).then_inc(s_y, 1)

        @block.vector
        def _(dve):
            v = Steps(dve, s_dve)
            dve.sem_inc(s_slot, RING)
            dve.sem_inc(s_ah, 1)
            dve.sem_inc(s_scr, 1)
            dve.wait_ge(s_idx, 32)
            for g in range(NG):
                nc.vector.tensor_copy(
                    idx_c[:, g * CPG:(g + 1) * CPG, :].rearrange("p c (t s) -> p c t s", t=2),
                    idx[:, 2 * g:2 * g + 2, :].rearrange("p t (c s) -> p c t s", s=CH)).then_inc(s_idc, 1)
            v.done(nc.vector.memset(ones[:, :], 1.0))
            v.done(nc.vector.memset(squeeze[:, :], 1.0))
            dve.wait_ge(s_idc, NG)
            v.done(nc.vector.tensor_scalar(kept[:, :, :], idx_c[:, :, :], 0.0, None, ALU.not_equal))
            v.done(nc.vector.tensor_scalar(masked[:, :, :], idx_c[:, :, :], 0.0, MASKED, ALU.is_equal, ALU.mult))
            dve.wait_ge(s_small, 16 * len(SMALL))
            v.done(nc.vector.tensor_copy(levels_f[:, :, :], levels_i[:, :, :]))
            v.wait()
            v.done(nc.vector.tensor_scalar(one_hot[:, :, :], levels_f[:, :, :], iota[:, 0:1], None, ALU.is_equal))
            ONE_HOT = v.n
            v.done(nc.vector.tensor_tensor(w_u[:, :], aw1[:, 0, :], aw1[:, 2, :], ALU.add))
            v.done(nc.vector.tensor_tensor(w_s[:, :], aw1[:, 1, :], aw1[:, 2, :], ALU.subtract))
            v.done(nc.vector.tensor_copy(w_p[:, :], aw1[:, 3, :]))
            dve.wait_ge(s_pro, 3)
            for t in range(NT):
                v.done(nc.vector.bn_stats(stats[:, t, :], pH[:, t * D:(t + 1) * D]))
            v.wait()
            for t in range(NT):
                v.done(nc.vector.bn_aggr(moments[:, t, :], stats[:, t, :]))
            v.wait()
            nc.vector.tensor_scalar(spread[:, :], moments[:, :, 1], EPS, None, ALU.add).then_inc(s_sqrt, 1)
            dve.wait_ge(s_sqrt, 2)
            v.done(nc.vector.reciprocal(spread[:, :], spread[:, :]))
            v.wait()
            for t in range(NT):
                v.done(nc.vector.tensor_scalar(img_hat[:, t, :], pH[:, t * D:(t + 1) * D], moments[:, t, 0:1],
                                               spread[:, t:t + 1], ALU.subtract, ALU.mult))
            IMG_HAT = v.n
            dve.wait_ge(s_pra, 6)
            v.done(nc.vector.tensor_tensor(target[:, :], fields[:, 2, :], fields[:, 3, :], ALU.add))
            TARGET = v.n
            dve.wait_ge(s_pro, 6)
            v.done(nc.vector.tensor_scalar(u_neg[:, :], pM[:, 0:NG * P], vec[:, R_AB1:R_AB1 + 1], -1.0,
                                           ALU.add, ALU.mult))
            U_NEG = v.n
            dve.wait_ge(s_pro, 7)
            v.done(nc.vector.tensor_scalar(c_row[:, :], pA[:, 0:NT], -1.0, ab2[:, 0:1], ALU.mult, ALU.add))
            v.wait()
            PRO.update(one_hot=ONE_HOT, img_hat=IMG_HAT, target=TARGET, u_neg=U_NEG)
            for g in range(NG):
                v.done(nc.vector.tensor_tensor(
                    shift[:, g * CPG:(g + 1) * CPG, :].rearrange("p c (t s) -> p c t s", t=2),
                    kept[:, g * CPG:(g + 1) * CPG, :].rearrange("p c (t s) -> p c t s", t=2),
                    c_row[:, 2 * g:2 * g + 2].unsqueeze(1).unsqueeze(3).broadcast_to([P, CPG, 2, CH]), ALU.mult))
            v.wait()
            v.done(nc.vector.tensor_tensor(shift[:, :, :], shift[:, :, :], masked[:, :, :], ALU.add))

            def start_group():
                v.done(nc.vector.memset(logit[:, 0, :, CH:CH + 1], LEAST))
                v.done(nc.vector.memset(total[:, :], 0.0))
                v.done(nc.vector.memset(hist[:, :, :], 0.0))
                v.wait()

            def chunk_product(n, g, r):
                dve.wait_ge(s_st, n + 2)
                nc.vector.tensor_tensor(
                    p_t[:, :].rearrange("p (t s b) -> p t s b", t=2, b=P),
                    s_t[:, :].rearrange("p (t s b) -> p t s b", t=2, b=P),
                    target[:, g * G:(g + 1) * G].rearrange("p (t b) -> p t b", t=2).unsqueeze(2)
                    .broadcast_to([P, 2, CH, P]), ALU.mult).then_inc(s_pt, 1)

            def chunk_relu(n, g):
                dve.wait_ge(s_h, n + 2)
                dve.wait_ge(s_sc, n + 1)
                nc.vector.tensor_tensor(
                    act_h[:, :].rearrange("p (s b) -> p s b", b=P), pH[:, 0:HALF_C].rearrange("p (s b) -> p s b", b=P),
                    u_neg[:, g * P:(g + 1) * P].unsqueeze(1).broadcast_to([P, CH, P]), ALU.max).then_inc(s_ah, 1)

            def chunk_max(n, r):
                dve.wait_ge(s_sc, n + 2)
                now, then = logit[:, r, :, :], logit[:, (r + 1) % RING, :, :]
                nc.vector.tensor_tensor(now[:, :, 0:CH], pM[:, 0:CW].rearrange("p (t s) -> p t s", t=2),
                                        kept[:, bass.ds(n, 1), :].rearrange("p a (t s) -> p (a t) s", t=2),
                                        ALU.mult).then_inc(s_scr, 1)
                dve.wait_ge(s_scr, n + 2)
                v.done(nc.vector.tensor_tensor(now[:, :, 0:CH], now[:, :, 0:CH],
                                               shift[:, bass.ds(n, 1), :].rearrange("p a (t s) -> p (a t) s", t=2),
                                               ALU.add))
                v.wait()
                v.done(nc.vector.tensor_reduce(then[:, :, CH:CH + 1], now, AX_X, ALU.max))
                v.wait()
                nc.vector.tensor_tensor(diff[:, :, :], now, then[:, :, CH:CH + 1].broadcast_to([P, 2, CH + 1]),
                                        ALU.subtract).then_inc(s_dif, 1)

            def chunk_rows(n, r):
                dve.wait_ge(s_exp, n + 1)
                v.done(nc.vector.tensor_tensor(hist[:, :, :], hist[:, :, :],
                                               exps[:, :, CH:CH + 1].broadcast_to([P, 2, D]), ALU.mult))
                v.done(nc.vector.tensor_tensor(total[:, :], total[:, :], exps[:, :, CH], ALU.mult))
                v.done(nc.vector.tensor_reduce(part_sum[:, :], exps[:, :, 0:CH], AX_X, ALU.add))
                v.wait()
                v.done(nc.vector.tensor_tensor(total[:, :], total[:, :], part_sum[:, :], ALU.add))
                for q in range(CW):
                    s, t = q // 2, q % 2
                    v.wait(1)
                    ins = nc.vector.scalar_tensor_tensor(
                        out=hist[:, t, :], in0=seq[:, r, t, s, :], scalar=exps[:, t, s:s + 1],
                        in1=hist[:, t, :], op0=ALU.mult, op1=ALU.add)
                    if q < CW - 1:
                        v.done(ins)
                    else:
                        ins.then_inc(s_slot, 1)

            def end_group(g):
                dve.wait_ge(s_slot, RING + CPG * (g + 1))
                v.wait()
                v.done(nc.vector.reciprocal(total[:, :], total[:, :]))
                v.wait()
                nc.vector.tensor_tensor(hist[:, :, :], hist[:, :, :],
                                        total[:, :].unsqueeze(2).broadcast_to([P, 2, D]), ALU.mult)\
                    .then_inc(s_hist, 1)

            def lo_part(to, of, hi):
                return nc.vector.tensor_tensor(to, of, hi, ALU.subtract)

            def squeezed(g):
                dve.wait_ge(s_sq, g + 1)
                nc.vector.tensor_scalar(squeeze[0:SE, :], pM[0:SE, 0:G], se_b1[:, 0:1], 0.0,
                                        ALU.add, ALU.max).then_inc(s_sqr, 1)

            def gated(g):
                dve.wait_ge(s_gr, g + 1)
                nc.vector.tensor_tensor(se[:, :, :], fields[:, :, g * G:(g + 1) * G], gate[:, :, :],
                                        ALU.mult).then_inc(s_se, 1)
                dve.wait_ge(s_dh, NF * g + 1)
                lo_part(xd[:, g, 1, 0:NF, :], se[:, :, :], f32(xd[:, g, 0, 0:NF, :])).then_inc(s_dl, 1)

            def products(g):
                at = NF
                for i in range(NV + 1):
                    if i < NV:
                        dve.wait_ge(s_vid, g + 1)
                        if i >= 2:
                            dve.wait_ge(s_dl, NF * g + i)
                        nc.vector.tensor_tensor(
                            prod[:, i % 2, 0:(NV - i) * G].rearrange("p (k n) -> p k n", n=G),
                            pH[:, i * G:(i + 1) * G].unsqueeze(1).broadcast_to([P, NV - i, G]), se[:, i + 1:NF, :],
                            ALU.mult).then_inc(s_pr, 1)
                    if i:
                        w = NV - i + 1
                        dve.wait_ge(s_dh, NF * g + i + 1)
                        lo_part(xd[:, g, 1, at:at + w, :],
                                prod[:, (i - 1) % 2, 0:w * G].rearrange("p (k n) -> p k n", n=G),
                                f32(xd[:, g, 0, at:at + w, :])).then_inc(s_dl, 1)
                        at += w

            def split_w(j, n, width=KT * P):
                dve.wait_ge(s_wh, n + 1)
                if not isinstance(n, int) or n >= 2:
                    dve.wait_ge(s_mm, n - 1)
                lo_part(w_lo[:, j, 0:width], w_raw[:, j, 0:width], f32(w_hi[:, j, 0:width])).then_inc(s_wl, 1)

            def whole(m, gs):
                v.done(nc.vector.tensor_tensor(by_group(dn, gs), f32(at_block(xd, 0, m, gs)),
                                               f32(at_block(xd, 1, m, gs)), ALU.add))

            def cross(l, m, j, n, gs):
                w = (gs.stop - gs.start) * G
                dve.wait_ge(s_mm, n + 1)
                v.wait()
                v.done(nc.vector.scalar_tensor_tensor(
                    out=xf[:, j, 0:w], in0=pA[:, j * BANK:j * BANK + w], scalar=vec[:, bass.ds(m + l * KT, 1)],
                    in1=dn[:, 0:w], op0=ALU.add, op1=ALU.mult))
                x = by_group(xf[:, j, :], gs)
                if l:
                    v.wait()
                    v.done(nc.vector.tensor_tensor(x, x, f32(at_block(xe, 0, m, gs)), ALU.add))
                term = f32(at_block(xe, 1, m, gs)) if l else by_group(dn, gs)
                v.wait()
                nc.vector.tensor_tensor(x, x, term, ALU.add).then_inc(s_xf[j], 1)

            def cross_lo(to, m, j, n, gs):
                dve.wait_ge(s_xh, n + 1)
                lo_part(at_block(to, 1, m, gs), by_group(xf[:, j, :], gs), f32(at_block(to, 0, m, gs)))\
                    .then_inc(s_xl, 1)

            def next_whole(j, turn, m, gs):
                dve.wait_ge(s_xf[j], turn + 1)
                whole(m, gs)

            start_group()
            for n in range(CPG):
                chunk_product(n, 0, n % RING)
                if n:
                    chunk_rows(n - 1, (n - 1) % RING)
                chunk_relu(n, 0)
                chunk_max(n, n % RING)
            chunk_rows(CPG - 1, RING - 1)
            end_group(0)
            dve.wait_ge(s_late, 16 * len(LATE))
            v.done(nc.vector.tensor_scalar(se1[:, :], se1_in[:, :], 1.0 / D, None, ALU.mult))
            nc.vector.tensor_copy(se2[:, :, :], se2_in[:, :].unsqueeze(2).broadcast_to([SE + 1, NF, P]))\
                .then_inc(s_hist, 1)
            for n in range(2):
                split_w(n, n)
            squeezed(0)
            gated(0)
            products(0)
            dve.wait_ge(s_hc, 1)
            start_group()
            dve.wait_ge(s_dl, NF)
            whole(0, groups(0))

            def after(n):
                gs = groups(n)
                cross(0, n, n % 2, n, gs)
                split_w(n % 2, n + 2)
                cross_lo(xe, n, n % 2, n, gs)
                if n + 1 < KT:
                    next_whole(n % 2, n // 2, n + 1, gs)

            for c in range(CPG):
                n, r, gs = CPG + c, c % RING, groups(0)
                if c:
                    cross(0, c - 1, (c - 1) % 2, c - 1, gs)
                chunk_product(n, 1, r)
                if c:
                    chunk_rows(n - 1, (c - 1) % RING)
                chunk_relu(n, 1)
                if c:
                    split_w((c + 1) % 2, c + 1)
                    cross_lo(xe, c - 1, (c - 1) % 2, c - 1, gs)
                    next_whole((c - 1) % 2, (c - 1) // 2, c, gs)
                chunk_max(n, r)
            chunk_rows(NG * CPG - 1, RING - 1)
            end_group(1)
            after(CPG - 1)
            after(CPG)
            after(CPG + 1)
            squeezed(1)
            after(CPG + 2)
            gated(1)
            after(CPG + 3)
            products(1)
            after(CPG + 4)

            gs = groups(L0B)
            dve.wait_ge(s_dl, NG * NF)
            next_whole((L0B - 1) % 2, (L0B - 1) // 2, 0, gs)
            cross(0, 0, 1, L0B, gs)
            split_w(1, L0B + 2)
            cross_lo(xe, 0, 1, L0B, gs)
            with dve.Fori(0, KT // 2) as i:
                v.enter(i, 4)
                for j in range(2):
                    n, m = 2 * i + j + L0B + 1, 2 * i + j + 1
                    next_whole(1 - j, i + L0B // 2 + j, m, gs)
                    cross(0, m, j, n, gs)
                    split_w(j, n + 2)
                    cross_lo(xe, m, j, n, gs)
                v.leave(KT // 2)
            gs = groups(L1)
            with dve.Fori(0, KT // 2 - 1) as i:
                v.enter(i, 6)
                for j in range(2):
                    n, m = 2 * i + j + L1, 2 * i + j
                    next_whole(1 - j, i + L1 // 2 - (1 - j), m, gs)
                    cross(1, m, j, n, gs)
                    split_w(j, n + 2)
                    cross_lo(xd, m, j, n, gs)
                v.leave(KT // 2 - 1)
            for n in range(MLP0 - 3, ITEMS - 2):
                if n < MLP0:
                    next_whole((n - 1) % 2, (n - 1) // 2, n - L1, gs)
                    cross(1, n - L1, n % 2, n, gs)
                split_w(n % 2, n + 2, KT * P if n + 2 < MLP0 else W1K * N1)
                if n < MLP0:
                    cross_lo(xd, n - L1, n % 2, n, gs)

            for t in range(NT):
                dve.wait_ge(s_w1, t + 1)
                v.done(nc.vector.bn_stats(stats[:, t, :], first_acc(t)))
                v.wait()
                v.done(nc.vector.bn_aggr(moments[:, t, :], stats[:, t, :]))
                v.wait()
                nc.vector.tensor_scalar(spread[:, t:t + 1], moments[:, t, 1:2], EPS, None, ALU.add).then_inc(s_var, 1)
                if t:
                    dve.wait_ge(s_pow, t)
                    nc.vector.tensor_scalar(hat1[:, t - 1, :], first_acc(t - 1), moments[:, t - 1, 0:1],
                                            spread[:, t - 1:t], ALU.subtract, ALU.mult).then_inc(s_hat, 1)
            dve.wait_ge(s_pow, NT)
            nc.vector.tensor_scalar(hat1[:, NT - 1, :], first_acc(NT - 1), moments[:, NT - 1, 0:1],
                                    spread[:, NT - 1:NT], ALU.subtract, ALU.mult).then_inc(s_hat, 1)
            for t in range(NT):
                dve.wait_ge(s_w2, t + 1)
                v.done(nc.vector.bn_stats(stats[:, t, :], second_acc(t)))
            v.wait()
            for t in range(NT):
                v.done(nc.vector.bn_aggr(moments[:, t, :], stats[:, t, :]))
            v.wait()
            dve.wait_ge(s_hat, NT)
            nc.vector.tensor_scalar(spread[:, :], moments[:, :, 1], EPS, None, ALU.add).then_inc(s_var, 1)
            dve.wait_ge(s_pow, NT + 1)
            for t in range(NT):
                ins = nc.vector.tensor_scalar(hat2[:, t, :], second_acc(t), moments[:, t, 0:1], spread[:, t:t + 1],
                                              ALU.subtract, ALU.mult)
            ins.then_inc(s_hat, 1)

        @block.tensor
        def _(pe):
            mm, tr = nc.tensor.matmul, nc.tensor.transpose
            pe.sem_inc(s_h, 1)
            pe.sem_inc(s_sc, 1)
            pe.wait_ge(s_small, 16 * len(SMALL))
            for t in range(NT):
                ins = tr(pT[:, t * P:(t + 1) * P], emb[:, t, :], ident[:, :])
            ins.then_inc(s_pro, 1)
            tr(pM[:, 0:NR], vec_rows[:, :], ident[0:NR, 0:NR])
            pe.wait_ge(s_dve, PRO["one_hot"])
            for j in range(2):
                ins = mm(pT[:, (1 + j) * BANK:(1 + j) * BANK + B], cate[:, :], one_hot[:, j, :], start=True, stop=True)
            ins.then_inc(s_pro, 1)
            pe.wait_ge(s_pra, 1)
            for t in range(NT):
                mm(pH[:, t * D:(t + 1) * D], ones[0:1, :], mm_b[0:1, :], start=True, stop=False)
                ins = mm(pH[:, t * D:(t + 1) * D], emb_t[:, t, :], mm_w[:, :], start=False, stop=True)
            ins.then_inc(s_pro, 1)
            pe.wait_ge(s_idr, 16 * NT)
            for t in range(NT):
                ins = tr(pT[:, t * P:(t + 1) * P], id_rows[:, t, :], ident[:, :])
            ins.then_inc(s_pro, 1)
            pe.wait_ge(s_dve, PRO["img_hat"])
            pe.wait_ge(s_pra, 4)
            for t in range(NT):
                ins = tr(pT[:, BANK + t * P:BANK + (t + 1) * P], img_hat[:, t, :], ident[:, :])
            ins.then_inc(s_pro, 1)
            pe.wait_ge(s_dve, PRO["target"])
            for t in range(NT):
                h, g = t % 2, t // 2
                ins = mm(pM[h * HID:(h + 1) * HID, g * P:(g + 1) * P], w_u[:, :], target[:, t * P:(t + 1) * P],
                         start=True, stop=True)
            ins.then_inc(s_pro, 1)
            pe.wait_ge(s_dve, PRO["u_neg"])
            for g in range(NG):
                ins = mm(pA[:, 2 * g:2 * g + 2], u_neg[:, g * P:(g + 1) * P], vec[:, R_AW2:R_AW2 + 2],
                         start=True, stop=True)
            ins.then_inc(s_pro, 1)

            def chunk_turn(n, r, turn):
                pe.wait_ge(s_rows[r], 16 * CW * (turn + 1))
                pe.wait_ge(s_st, n + 1)
                for q in range(CW):
                    ins = tr(pT[:, q * P:(q + 1) * P], seq[:, r, q // CH, q % CH, :], ident[:, :])
                ins.then_inc(s_tr, 1)

            def chunk_hidden(n):
                pe.wait_ge(s_pt, n + 1)
                pe.wait_ge(s_ah, n + 1)
                for s0, ns in ((0, 4), (4, CH - 4)):
                    for w, x in ((w_s, s_t), (w_p, p_t)):
                        for h in range(2):
                            at = (h * CH + s0) * P
                            ins = mm(pH[h * HID:(h + 1) * HID, s0 * P:(s0 + ns) * P], w[:, :],
                                     x[:, at:at + ns * P], start=(w is w_s), stop=(w is w_p))
                ins.then_inc(s_h, 1)

            def chunk_scores(n):
                pe.wait_ge(s_ah, n + 2)
                pe.wait_ge(s_scr, n + 1)
                for s in range(CH):
                    ins = mm(pM[:, s:s + CH + 1:CH], act_h[:, s * P:(s + 1) * P], vec[:, R_AW2:R_AW2 + 2],
                             start=True, stop=True)
                ins.then_inc(s_sc, 1)

            def hist_turn(g):
                pe.wait_ge(s_hist, 2 * g + 1)
                for t in range(2):
                    ins = tr(pM[:, t * P:(t + 1) * P], hist[:, t, :], ident[:, :])
                ins.then_inc(s_ht, 1)

            def squeeze_sum(g):
                pe.wait_ge(s_hist, 2)
                pe.wait_ge(s_hc, g + 1)
                for f in range(NF):
                    ins = mm(pM[0:SE, 0:G], se1[:, f * SE:(f + 1) * SE], fields[:, f, g * G:(g + 1) * G],
                             start=(f == 0), stop=(f == NF - 1))
                ins.then_inc(s_sq, 1)

            def gate_sum(g):
                pe.wait_ge(s_sqr, g + 1)
                for f in range(NF):
                    ins = mm(pT[:, f * G:(f + 1) * G], se2[:, f, :], squeeze[:, :], start=True, stop=True)
                ins.then_inc(s_ga, 1)

            def vids(g):
                pe.wait_ge(s_se, g + 1)
                for f in range(NV):
                    ins = mm(pH[:, f * G:(f + 1) * G], bil_w[:, f, :], se[:, f, :], start=True, stop=True)
                ins.then_inc(s_vid, 1)

            PARTS = [0]
            for i in range(NV):
                PARTS.append(PARTS[-1] + (NF if i == 0 else NV - i + 1))

            def block(j, x, n, gs, ks, turn, last_lo=None, parts=None):
                if ks.start == 0:
                    pe.wait_ge(s_wl, n + 1)
                    if not isinstance(n, int) or n >= 2:
                        pe.wait_ge(s_xf[j], turn)
                acc = by_group(pA[:, j * BANK:(j + 1) * BANK], gs)
                for k in ks:
                    if last_lo and k == KT - 1:
                        pe.wait_ge(s_xl, last_lo)
                    if parts is not None and k in PARTS:
                        pe.wait_ge(s_dl, NF * parts + PARTS.index(k) + 1)
                    hi, lo = w_hi[:, j, k * P:(k + 1) * P], w_lo[:, j, k * P:(k + 1) * P]
                    mm(acc, hi, x[:, gs, 0, k, :], start=(k == 0), stop=False)
                    mm(acc, hi, x[:, gs, 1, k, :], start=False, stop=False)
                    ins = mm(acc, lo, x[:, gs, 0, k, :], start=False, stop=(k == KT - 1))
                if ks.stop == KT:
                    ins.then_inc(s_mm, 1)

            ALL = range(KT)
            with pe.Fori(0, CPG // RING) as i:
                for r in range(RING):
                    chunk_turn(i * RING + r, r, i)
                    chunk_hidden(i * RING + r)
                    chunk_scores(i * RING + r)
            hist_turn(0)
            squeeze_sum(0)
            gate_sum(0)
            vids(0)
            gs = groups(0)
            for c in range(CPG):
                parts = 0 if c == 0 else None
                if c == 0:
                    pe.wait_ge(s_gr, 1)
                chunk_turn(CPG + c, c % RING, CPG // RING + c // RING)
                block(c % 2, xd, c, gs, range(0, KT // 2 + 1), c // 2, parts=parts)
                chunk_hidden(CPG + c)
                block(c % 2, xd, c, gs, range(KT // 2 + 1, KT), c // 2, parts=parts)
                chunk_scores(CPG + c)
            for q, step in enumerate((hist_turn, squeeze_sum, gate_sum, vids, None)):
                block((CPG + q) % 2, xd, CPG + q, gs, ALL, (CPG + q) // 2)
                if step:
                    step(1)
            gs = groups(L0B)
            block(1, xd, L0B, gs, ALL, L0B // 2, parts=1)
            with pe.Fori(0, KT // 2) as i:
                for j in range(2):
                    block(j, xd, 2 * i + j + L0B + 1, gs, ALL, i + (L0B + 1) // 2)
            gs = groups(L1)
            pe.wait_ge(s_xl, L1 - 1)
            block(0, xe, L1, gs, ALL, L1 // 2, last_lo=L1)
            with pe.Fori(0, KT // 2) as i:
                for j in range(2):
                    block(1 - j, xe, 2 * i + j + L1 + 1, gs, ALL, i + (L1 + 1 + j) // 2)

            for t in range(NT):
                mm(first_acc(t), ones[0:1, :], b1[0:1, :], start=True, stop=False)
            for q in range(NW1):
                n = MLP0 + q
                last = q == NW1 - 1
                pe.wait_ge(s_wl, n + 1)
                pe.wait_ge(s_xl, L1 + (q + 1) * W1K)
                order = [(k, t) for t in range(NT) for k in range(W1K)] if last else \
                    [(k, t) for k in range(W1K) for t in range(NT)]
                for k, t in order:
                    hi = w_hi[:, n % 2, k * N1:(k + 1) * N1]
                    lo = w_lo[:, n % 2, k * N1:(k + 1) * N1]
                    kk = q * W1K + k
                    x_hi = xd[:, t // 2, 0, kk, (t % 2) * P:(t % 2) * P + P]
                    x_lo = xd[:, t // 2, 1, kk, (t % 2) * P:(t % 2) * P + P]
                    mm(first_acc(t), x_hi, hi, start=False, stop=False)
                    mm(first_acc(t), x_hi, lo, start=False, stop=False)
                    ins = mm(first_acc(t), x_lo, hi, start=False, stop=(kk == KT - 1))
                    if last and k == W1K - 1:
                        ins.then_inc(s_w1, 1)
                if not last:
                    ins.then_inc(s_mm, 1)

            def turn_rows(hat, c, n, have):
                if have:
                    pe.wait_ge(s_ge, have)
                to, o = (pM, 0) if c % 2 else (pH, BANK)
                for t in range(NT):
                    if n == 0 and c == 0:
                        pe.wait_ge(s_hat, t + 1)
                    ins = tr(to[:, o + t * P:o + (t + 1) * P], hat[:, t, c * P:(c + 1) * P], ident[:, :])
                ins.then_inc(s_mt, 1)

            turn_rows(hat1, 0, 0, 0)
            turn_rows(hat1, 1, 0, 0)
            for j in range(2):
                pe.wait_ge(s_xf[j], (MLP0 + 1 - j) // 2)
            for t in range(NT):
                mm(second_acc(t), ones[0:1, :], b2[0:1, :], start=True, stop=False)
            for c in range(K1):
                pe.wait_ge(s_ge, c + 1)
                for t in range(NT):
                    ins = mm(second_acc(t), h1_t[:, c, t * P:(t + 1) * P], w2[:, c, :], start=False,
                             stop=(c == K1 - 1))
                    if c == K1 - 1:
                        ins.then_inc(s_w2, 1)
                if c + 2 < K1:
                    turn_rows(hat1, c + 2, 0, c + 1)
            pe.wait_ge(s_hat, NT + 1)
            for c in range(K2):
                turn_rows(hat2, c, 1, K1)
            for c in range(K2):
                pe.wait_ge(s_ge, K1 + c + 1)
                ins = mm(pH[0:1, 0:B], vec[:, R_W3 + c:R_W3 + c + 1], h2_t[:, c, :], start=(c == 0), stop=(c == K2 - 1))
            ins.then_inc(s_w3, 1)


def kernel(**inputs):
    import numpy as np
    import concourse.bacc as bacc
    from concourse.bass_utils import run_bass_kernel_spmd

    nc = bacc.Bacc("TRN2", target_bir_lowering=False, num_devices=1)
    arrays, aps = {}, {}
    for name in INS:
        arr = np.ascontiguousarray(inputs[name])
        arrays[f"in_{name}"] = arr
        aps[name] = nc.dram_tensor(f"in_{name}", arr.shape, mybir.dt.from_np(arr.dtype), kind="ExternalInput").ap()
    consts = {"ident": np.eye(P, dtype=np.float32),
              "iota": np.arange(inputs['L0_rec_cate_table'].shape[0], dtype=np.float32).reshape(-1, 1)}
    for name, arr in consts.items():
        arrays[f"in_{name}"] = arr
        aps[name] = nc.dram_tensor(f"in_{name}", arr.shape, F32, kind="ExternalInput").ap()
    B = inputs['r_item_id'].shape[0]
    out = nc.dram_tensor("out_y", (B,), F32, kind="ExternalOutput").ap()
    build(nc, aps, aps["ident"], aps["iota"], out)
    r = run_bass_kernel_spmd(nc, [arrays], core_ids=[0])
    return r.results[0]["out_y"]
```

```python
from contextlib import ExitStack

import concourse.bass as bass
from concourse import mybir

F32 = mybir.dt.float32
F32R = mybir.dt.float32r
I32 = mybir.dt.int32
ALU = mybir.AluOpType
ACT = mybir.ActivationFunctionType
AX_X = mybir.AxisListType.X

P = 128
BANK = 512
EPS = 1e-5
MASKED = -1000000000.0
LEAST = -3.0e38

INS = ['r_item_emb_d128', 'r_item_id', 'r_likes_level', 'r_views_level', 'r_item_seq',
       'L0_rec_item_table', 'L0_rec_cate_table', 'L0_rec_mm_w', 'L0_rec_mm_b', 'L0_rec_mm_ln_g',
       'L0_rec_mm_ln_b', 'L0_rec_aw1', 'L0_rec_ab1', 'L0_rec_aw2', 'L0_rec_ab2', 'L0_rec_se_w1',
       'L0_rec_se_b1', 'L0_rec_se_w2', 'L0_rec_se_b2', 'L0_rec_bil_W', 'L0_rec_cross_K',
       'L0_rec_cross_bias', 'L0_rec_w1', 'L0_rec_b1', 'L0_rec_ln1g', 'L0_rec_ln1b', 'L0_rec_w2',
       'L0_rec_b2', 'L0_rec_ln2g', 'L0_rec_ln2b', 'L0_rec_w3', 'L0_rec_b3']


class Steps:

    def __init__(self, eng, sem):
        self.eng, self.sem, self.n, self.i, self.per = eng, sem, 0, None, 0

    def done(self, instruction):
        instruction.then_inc(self.sem, 1)
        self.n += 1

    def wait(self, behind=0):
        n = self.n - behind
        self.eng.wait_ge(self.sem, n if self.i is None else self.i * self.per + n)

    def enter(self, i, per):
        self.i, self.per, self.start = i, per, self.n

    def leave(self, trips):
        assert self.n - self.start == self.per, (self.n - self.start, self.per)
        self.n = self.start + self.per * trips
        self.i = None


def build(nc, a, ident_in, iota_in, out):
    B, S = a['r_item_seq'].shape
    D = a['L0_rec_item_table'].shape[1]
    LV = a['L0_rec_cate_table'].shape[0]
    HID = a['L0_rec_aw1'].shape[1]
    NF, SE = a['L0_rec_se_w1'].shape
    NL, TD, _ = a['L0_rec_cross_K'].shape
    N1 = a['L0_rec_w1'].shape[1]
    N2 = a['L0_rec_w2'].shape[1]
    NT = B // P
    NG = NT // 2
    G = 2 * P
    CH = 5
    CPG = S // CH
    RING = CPG // 2
    CW = 2 * CH
    HALF_C = CH * P
    KT = TD // P
    NV = NF - 1
    W1K = 3
    NW1 = KT // W1K
    K1 = N1 // P
    K2 = N2 // P
    assert D == P and 2 * HID == P and B == 4 * P and S % 10 == 0 and NL == 2
    assert KT % 2 == 1 and NW1 * W1K == KT and KT >= CPG + 5 and K2 == 2
    L0B, L1, MLP0 = KT, 2 * KT, 3 * KT
    ITEMS = MLP0 + NW1

    R_CB, R_G1 = 0, NL * KT
    R_B1 = R_G1 + K1
    R_G2 = R_B1 + K1
    R_B2 = R_G2 + K2
    R_MG = R_B2 + K2
    R_MB = R_MG + 1
    R_W3 = R_MB + 1
    R_AB1 = R_W3 + K2
    R_AW2 = R_AB1 + 1
    NR = R_AW2 + 2

    ctx = ExitStack()
    with ctx:
        def sb(name, shape, dt=F32, at=ctx):
            return at.enter_context(nc.sbuf_tensor(name, shape, dt))

        def ps(name, shape):
            return ctx.enter_context(nc.psum_tensor(name, shape, F32))

        def sem(name):
            return ctx.enter_context(nc.semaphore(name))

        PART = 2 * KT * G
        with ExitStack() as early:
            used = [0]

            def eb(name, shape, dt=F32):
                n = 1
                for x in shape[1:]:
                    n *= x
                used[0] += n
                return sb(name, shape, dt, early)

            def fill(name, parts):
                eb(name, [P, parts * PART - used[0]])

            emb = eb("emb", [P, NT, D])
            emb_t = eb("emb_t", [P, NT, P])
            img_hat = eb("img_hat", [P, NT, D])
            id_rows = eb("id_rows", [P, NT, D])
            levels_i = eb("levels_i", [LV, 2, B], I32)
            levels_f = eb("levels_f", [LV, 2, B])
            one_hot = eb("one_hot", [LV, 2, B])
            vec_rows = eb("vec_rows", [NR, P])
            aw1 = eb("aw1", [P, 4, HID])
            mm_w = eb("mm_w", [P, D])
            cate = eb("cate", [LV, D])
            mm_b = eb("mm_b", [1, D])
            idx = eb("idx", [P, NT, S], I32)
            masked = eb("masked", [P, NG * CPG, CW])
            fill("fill_xd0", 1)
            seq = eb("seq", [P, RING, 2, CH, D])
            s_t = eb("s_t", [P, CW * P])
            with ExitStack() as mlp:
                hat1 = sb("hat1", [P, NT, N1], F32, mlp)
                h1_t = sb("h1_t", [P, K1, B], F32, mlp)
                hat2 = sb("hat2", [P, NT, N2], F32, mlp)
                h2_t = sb("h2_t", [P, K2, B], F32, mlp)
            fill("fill_xe0", 3)
            p_t = eb("p_t", [P, CW * P])
            se = eb("se", [P, NF, G])
            gate = eb("gate", [P, NF, G])
            prod = eb("prod", [P, 2, NV * G])
            weighed = eb("weighed", [P, CH, 2, D])
        xd = sb("xd", [P, NG, 2, KT, G], F32R)
        xe = sb("xe", [P, NG, 2, KT, G], F32R)
        target = sb("target", [P, B])
        u_neg = sb("u_neg", [P, NG * P])
        act_h = sb("act_h", [P, HALF_C])
        dn = sb("dn", [P, B])
        xf = sb("xf", [P, 2, B])
        w_raw = sb("w_raw", [P, 2, KT * P])
        w_hi = sb("w_hi", [P, 2, KT * P], F32R)
        w_lo = sb("w_lo", [P, 2, KT * P], F32R)
        fields = sb("fields", [P, NF, B])
        ident = sb("ident", [P, P])
        iota = sb("iota", [LV, 1])
        vec = sb("vec", [P, NR])
        w_u = sb("w_u", [P, HID])
        w_s = sb("w_s", [P, HID])
        w_p = sb("w_p", [P, HID])
        bil_w = sb("bil_w", [P, NV, D])
        w2 = sb("w2", [P, K1, N2])
        ones = sb("ones", [1, P])
        b1 = sb("b1", [1, N1])
        b2 = sb("b2", [1, N2])
        ab2 = sb("ab2", [P, 1])
        b3 = sb("b3", [P, 1])
        se1_in = sb("se1_in", [P, NF * SE])
        se1 = sb("se1", [P, NF * SE])
        se_b1 = sb("se_b1", [SE, 1])
        se2_in = sb("se2_in", [SE + 1, NF])
        se2 = sb("se2", [SE + 1, NF, P])
        squeeze = sb("squeeze", [SE + 1, G])
        idx_c = sb("idx_c", [P, NG * CPG, CW], I32)
        idx_g = sb("idx_g", [P, RING, CW], I32)
        ids = sb("ids", [P, NT], I32)
        kept = sb("kept", [P, NG * CPG, CW])
        shift = sb("shift", [P, NG * CPG, CW])
        c_row = sb("c_row", [P, NT])
        logit = sb("logit", [P, RING, 2, CH + 1])
        diff = sb("diff", [P, 2, CH + 1])
        exps = sb("exps", [P, 2, CH + 1])
        total = sb("total", [P, 2])
        part_sum = sb("part_sum", [P, 2])
        hist = sb("hist", [P, 2, D])
        stats = sb("stats", [P, NT, 6])
        moments = sb("moments", [P, NT, 2])
        spread = sb("spread", [P, NT])
        minus_half = sb("minus_half", [P, 1])
        y_cols = sb("y_cols", [P, NT])
        y = sb("y", [NT, P])

        pT = ps("pT", [P, 3 * BANK])
        pH = ps("pH", [P, 2 * BANK])
        pM = ps("pM", [P, BANK])
        pA = ps("pA", [P, 2 * BANK])

        s_idx = sem("idx_loaded")
        s_idc = sem("idx_by_chunk")
        s_small = sem("small_loaded")
        s_late = sem("late_loaded")
        s_idr = sem("id_rows_landed")
        s_idxg = sem("idx_chunk_ready")
        s_seen = sem("idx_chunk_seen")
        s_rows = [sem(f"rows_landed{r}") for r in range(RING)]
        s_slot = sem("ring_slots_free")
        s_raw = [sem(f"w_raw_landed{j}") for j in range(2)]
        s_out = sem("out_stored")
        s_vz = sem("vec_rows_zeroed")
        s_pro = sem("prologue_pe")
        s_pra = sem("prologue_act")
        s_dve = sem("dve_step")
        s_sqrt = sem("roots_taken")
        s_tr = sem("chunk_transposed")
        s_st = sem("s_t_ready")
        s_h = sem("hidden_done")
        s_ah = sem("act_h_ready")
        s_sc = sem("scores_done")
        s_scr = sem("scores_read")
        s_pt = sem("p_t_ready")
        s_dif = sem("diff_ready")
        s_exp = sem("exps_ready")
        s_wgh = sem("rows_weighed")
        s_hist = sem("hist_ready")
        s_ht = sem("hist_transposed")
        s_hc = sem("hist_copied")
        s_sq = sem("squeeze_summed")
        s_sqr = sem("squeeze_ready")
        s_ga = sem("gate_summed")
        s_gr = sem("gate_ready")
        s_se = sem("se_ready")
        s_vid = sem("vids_done")
        s_pr = sem("prod_ready")
        s_dh = sem("xd_hi_ready")
        s_dl = sem("xd_lo_ready")
        s_wh = sem("w_hi_ready")
        s_wl = sem("w_lo_ready")
        s_mm = sem("block_done")
        s_xf = [sem(f"xf_ready{j}") for j in range(2)]
        s_xh = sem("x_hi_ready")
        s_xl = sem("x_lo_ready")
        s_w1 = sem("w1_done")
        s_var = sem("variances_ready")
        s_pow = sem("spreads_ready")
        s_hat = sem("hats_ready")
        s_mt = sem("mlp_transposed")
        s_ge = sem("gelu_done")
        s_w2 = sem("w2_done")
        s_w3 = sem("w3_done")
        s_yc = sem("y_columns_ready")
        s_yt = sem("y_turned")
        s_y = sem("y_ready")

        def f32(ap):
            return ap.bitcast(F32)

        K = a['L0_rec_cross_K'].rearrange("l (k p) n -> l p k n", p=P)
        W1 = a['L0_rec_w1'].rearrange("(k p) n -> p k n", p=P)
        W2 = a['L0_rec_w2'].rearrange("(k p) n -> p k n", p=P)

        def row(name, n=1):
            return a[name].rearrange("(a n) -> a n", a=n)

        SMALL, LATE = [], []

        def groups(n_first):
            return slice(0, 1) if n_first < L0B else slice(1, 2) if n_first < L1 else slice(0, 2)

        def at_block(x, h, m, gs):
            return x[:, gs, h, bass.ds(m, 1), :].rearrange("p g a n -> p g (a n)")

        def by_group(x, gs):
            n = gs.stop - gs.start
            return x[:, 0:n * G].rearrange("p (g n) -> p g n", g=n)

        def first_acc(t):
            return pT[:, t * BANK:t * BANK + N1] if t < 3 else pH[:, 0:N1]

        def second_acc(t):
            return pA[:, t * BANK:t * BANK + N2] if t < 2 else pT[:, (t - 2) * BANK:(t - 2) * BANK + N2]

        PARTS = [0, NF]
        for i in range(NV - 1):
            PARTS.append(PARTS[-1] + NV - i)

        GELUS = [(l, h, c) for l, k in ((0, K1), (1, K2)) for h in range(2) for c in range(k)]

        def turned(q):
            return pM[:, 0:G] if q % 2 else pH[:, BANK:BANK + G]

        PRO = {}

        block = ctx.enter_context(nc.Block())

        @block.sync
        def _(sp):
            sp.dma_start(idx[:, :, :], a['r_item_seq'].rearrange("(t p) s -> p t s", p=P)).then_inc(s_idx, 16)
            sp.dma_start(ids[:, :], a["r_item_id"].rearrange("(t p) -> p t", p=P),
                         allow_slow_non_contiguous=True).then_inc(s_idx, 16)

            def small(to, of):
                sp.dma_start(to, of).then_inc(s_small, 16)
                SMALL.append(1)

            def late(to, of):
                sp.dma_start(to, of).then_inc(s_late, 16)
                LATE.append(1)

            small(emb[:, :, :], a['r_item_emb_d128'].rearrange("(t p) d -> p t d", p=P))
            small(ident[:, :], ident_in)
            small(mm_w[:, :], a['L0_rec_mm_w'])
            small(mm_b[:, :], row('L0_rec_mm_b'))
            small(iota[:, :], iota_in)
            small(cate[:, :], a['L0_rec_cate_table'])
            for j, name in enumerate(('r_likes_level', 'r_views_level')):
                small(levels_i[:, j, :], row(name).broadcast_to([LV, B]))
            small(aw1[:, :, :], a['L0_rec_aw1'].rearrange("(q p) n -> p q n", p=P))
            sp.wait_ge(s_vz, 1)
            small(vec_rows[R_CB:R_G1, :], a['L0_rec_cross_bias'].rearrange("l (m p) -> (l m) p", p=P))
            small(vec_rows[R_G1:R_B1, :], row('L0_rec_ln1g', K1))
            small(vec_rows[R_B1:R_G2, :], row('L0_rec_ln1b', K1))
            small(vec_rows[R_G2:R_B2, :], row('L0_rec_ln2g', K2))
            small(vec_rows[R_B2:R_MG, :], row('L0_rec_ln2b', K2))
            small(vec_rows[R_MG:R_MB, :], row('L0_rec_mm_ln_g'))
            small(vec_rows[R_MB:R_W3, :], row('L0_rec_mm_ln_b'))
            small(vec_rows[R_W3:R_AB1, :], a['L0_rec_w3'].rearrange("(c p) a -> c (p a)", p=P))
            for h in range(2):
                small(vec_rows[R_AB1:R_AB1 + 1, h * HID:(h + 1) * HID], row('L0_rec_ab1'))
                small(vec_rows[R_AW2 + h:R_AW2 + h + 1, h * HID:(h + 1) * HID],
                      a['L0_rec_aw2'].rearrange("p a -> a p"))
            small(ab2[:, :], row('L0_rec_ab2').broadcast_to([P, 1]))
            late(se1_in[:, :], a['L0_rec_se_w1'].rearrange("(a f) i -> a (f i)", a=1).broadcast_to([P, NF * SE]))
            late(se_b1[:, :], a['L0_rec_se_b1'].rearrange("(p a) -> p a", a=1))
            late(se2_in[0:SE, :], a['L0_rec_se_w2'])
            late(se2_in[SE:SE + 1, :], row('L0_rec_se_b2'))
            late(bil_w[:, :, :], a['L0_rec_bil_W'].rearrange("f d e -> d f e"))
            late(b1[:, :], row('L0_rec_b1'))
            late(b2[:, :], row('L0_rec_b2'))
            late(b3[:, :], row('L0_rec_b3').broadcast_to([P, 1]))
            late(w2[:, :, :], W2)

            def load_block(l, m, n, j):
                sp.wait_ge(s_wl, n - 1)
                sp.dma_start(w_raw[:, j, :].rearrange("p (k n) -> p k n", k=KT),
                             K[l, :, :, bass.ds(m * P, P)]).then_inc(s_raw[j], 16)

            for j in range(2):
                sp.dma_start(w_raw[:, j, :].rearrange("p (k n) -> p k n", k=KT),
                             K[0, :, :, j * P:(j + 1) * P]).then_inc(s_raw[j], 16)
            with sp.Fori(0, (KT - 3) // 2) as i:
                for j in range(2):
                    load_block(0, 2 * i + 2 + j, 2 * i + 2 + j, j)
            load_block(0, KT - 1, KT - 1, 0)
            load_block(0, 0, L0B, 1)
            with sp.Fori(0, KT // 2) as i:
                for j in range(2):
                    load_block(0, 2 * i + 1 + j, 2 * i + 1 + j + L0B, j)
            with sp.Fori(0, KT // 2) as i:
                for j in range(2):
                    load_block(1, 2 * i + j, 2 * i + j + L1, j)
            load_block(1, KT - 1, MLP0 - 1, 0)
            for q in range(NW1):
                n = MLP0 + q
                sp.wait_ge(s_wl, n - 1)
                sp.dma_start(w_raw[:, n % 2, 0:W1K * N1].rearrange("p (k n) -> p k n", k=W1K),
                             W1[:, q * W1K:(q + 1) * W1K, :]).then_inc(s_raw[n % 2], 16)
            sp.wait_ge(s_y, 1)
            sp.dma_start(out.rearrange("(t p) -> t p", p=P), y[:, :]).then_inc(s_out, 16)
            sp.wait_ge(s_out, 16)

        @block.gpsimd
        def _(pool):
            nc.gpsimd.memset(vec_rows[:, :], 0.0).then_inc(s_vz, 1)
            nc.gpsimd.memset(minus_half[:, :], -0.5).then_inc(s_vz, 1)
            pool.wait_ge(s_idx, 32)
            table = a['L0_rec_item_table']
            for t in range(NT):
                nc.gpsimd.indirect_dma_start(
                    id_rows[:, t, :], None, table,
                    bass.IndirectOffsetOnAxis(ap=ids[:, t:t + 1], axis=0)).then_inc(s_idr, 16)
            with pool.Fori(0, NG * CPG // RING) as i:
                for r in range(RING):
                    pool.wait_ge(s_slot, i * RING + r + 1)
                    pool.wait_ge(s_idxg, i * RING + r + 1)
                    pool.sem_inc(s_seen, 1)
                    for q in range(CW):
                        nc.gpsimd.indirect_dma_start(
                            seq[:, r, q // CH, q % CH, :], None, table,
                            bass.IndirectOffsetOnAxis(ap=idx_g[:, r, q:q + 1], axis=0)).then_inc(s_rows[r], 16)

            pool.wait_ge(s_vz, 2)
            for n in range(2 * NT):
                pool.wait_ge(s_var, n + 1)
                col = spread[:, n % NT:n % NT + 1]
                nc.gpsimd.tensor_tensor(col, col, minus_half[:, :], ALU.pow).then_inc(s_pow, 1)

        @block.scalar
        def _(act):
            act.sem_inc(s_st, 1)
            act.wait_ge(s_pro, 1)
            nc.scalar.copy(emb_t[:, :, :], pT[:, 0:B]).then_inc(s_pra, 1)
            act.wait_ge(s_pro, 2)
            nc.scalar.copy(vec[:, :], pM[:, 0:NR]).then_inc(s_pra, 1)
            for j in range(2):
                nc.scalar.copy(fields[:, j, :], pT[:, (1 + j) * BANK:(1 + j) * BANK + B]).then_inc(s_pra, 1)
            act.wait_ge(s_pro, 4)
            nc.scalar.copy(fields[:, 2, :], pT[:, 0:B]).then_inc(s_pra, 1)
            act.wait_ge(s_sqrt, 1)
            nc.scalar.activation(spread[:, :], spread[:, :], ACT.Sqrt).then_inc(s_sqrt, 1)
            act.wait_ge(s_pro, 5)
            act.wait_ge(s_pra, 2)
            nc.scalar.activation(fields[:, 3, :], pT[:, BANK:BANK + B], ACT.Gelu,
                                 scale=vec[:, R_MG:R_MG + 1], bias=vec[:, R_MB:R_MB + 1]).then_inc(s_pra, 1)

            def chunk_copy(n):
                act.wait_ge(s_tr, n + 1)
                act.wait_ge(s_h, n + 1)
                nc.scalar.copy(s_t[:, :], pT[:, 0:CW * P]).then_inc(s_st, 1)

            def chunk_exp(n):
                act.wait_ge(s_dif, n + 1)
                nc.scalar.activation(exps[:, :, :], diff[:, :, :], ACT.Exp).then_inc(s_exp, 1)

            def chunk_weigh(n, r):
                act.wait_ge(s_exp, n + 1)
                for s in range(CH):
                    for t in range(2):
                        ins = nc.scalar.activation(weighed[:, s, t, :], seq[:, r, t, s, :], ACT.Copy,
                                                   scale=exps[:, t, s:s + 1])
                ins.then_inc(s_wgh, 1)
                act.wait_ge(s_wgh, n - CPG + 1)
                act.sem_inc(s_slot, 1)

            def split_w(j, n, turn, width=KT * P):
                act.wait_ge(s_raw[j], 16 * turn)
                if not isinstance(n, int) or n >= 2:
                    act.wait_ge(s_mm, n - 1)
                nc.scalar.copy(w_hi[:, j, 0:width], w_raw[:, j, 0:width]).then_inc(s_wh, 1)

            def split_x(to, m, j, turn, gs):
                act.wait_ge(s_xf[j], turn + 1)
                nc.scalar.copy(at_block(to, 0, m, gs), by_group(xf[:, j, :], gs)).then_inc(s_xh, 1)

            def after(n):
                split_w(n % 2, n + 2, (n + 2) // 2 + 1)
                split_x(xe, n, n % 2, n // 2, groups(n))

            for n in range(2):
                split_w(n, n, 1)
            with act.Fori(0, CPG // RING) as i:
                for r in range(RING):
                    n = i * RING + r
                    if r == 0:
                        chunk_copy(n)
                    if r + 1 < RING:
                        chunk_copy(n + 1)
                    chunk_exp(n)
            chunk_copy(CPG)

            def hist_out(g):
                act.wait_ge(s_ht, g + 1)
                nc.scalar.copy(fields[:, NF - 1, g * G:(g + 1) * G], pM[:, 0:G]).then_inc(s_hc, 1)

            def gates(g):
                act.wait_ge(s_ga, g + 1)
                nc.scalar.activation(gate[:, :, :], pT[:, 0:NF * G].rearrange("p (f n) -> p f n", f=NF),
                                     ACT.Sigmoid).then_inc(s_gr, 1)

            def fields_hi(g):
                act.wait_ge(s_se, g + 1)
                nc.scalar.copy(xd[:, g, 0, 0:NF, :], se[:, :, :]).then_inc(s_dh, 1)

            def products_hi(g, fs):
                for i in fs:
                    at = PARTS[i + 1]
                    act.wait_ge(s_pr, NV * g + i + 1)
                    nc.scalar.copy(xd[:, g, 0, at:at + NV - i, :],
                                   prod[:, i % 2, 0:(NV - i) * G].rearrange("p (k n) -> p k n", n=G))\
                        .then_inc(s_dh, 1)

            hist_out(0)
            gates(0)
            fields_hi(0)
            products_hi(0, range(0, 2))
            chunk_copy(CPG + 1)
            products_hi(0, range(2, NV))
            chunk_exp(CPG)
            chunk_weigh(CPG, 0)
            for c in range(1, CPG):
                split_w((c + 1) % 2, c + 1, (c + 1) // 2 + 1)
                if c + 1 < CPG:
                    chunk_copy(CPG + c + 1)
                split_x(xe, c - 1, (c - 1) % 2, (c - 1) // 2, groups(c - 1))
                chunk_exp(CPG + c)
                chunk_weigh(CPG + c, c % RING)
            after(CPG - 1)
            hist_out(1)
            after(CPG)
            after(CPG + 1)
            gates(1)
            fields_hi(1)
            after(CPG + 2)
            products_hi(1, range(0, 2))
            after(CPG + 3)
            products_hi(1, range(2, NV))
            after(CPG + 4)
            gs = groups(L0B)
            split_w(1, L0B + 2, (L0B + 2) // 2 + 1)
            split_x(xe, 0, 1, L0B // 2, gs)
            with act.Fori(0, KT // 2) as i:
                for j in range(2):
                    split_w(j, 2 * i + j + L0B + 3, i + (L0B + 3) // 2 + 1)
                    split_x(xe, 2 * i + j + 1, j, i + (L0B + 1) // 2, gs)
            gs = groups(L1)
            with act.Fori(0, KT // 2 - 1) as i:
                for j in range(2):
                    split_w(j, 2 * i + j + L1 + 2, i + L1 // 2 + 2)
                    split_x(xd, 2 * i + j, j, i + L1 // 2, gs)
            for n in range(MLP0 - 3, ITEMS - 2):
                split_w(n % 2, n + 2, (n + 2) // 2 + 1, KT * P if n + 2 < MLP0 else W1K * N1)
                if n < MLP0:
                    split_x(xd, n - L1, n % 2, n // 2, gs)

            for q, (l, h, c) in enumerate(GELUS):
                to, g0, b0 = ((h1_t, R_G1, R_B1), (h2_t, R_G2, R_B2))[l]
                act.wait_ge(s_mt, q + 1)
                nc.scalar.activation(to[:, c, h * G:(h + 1) * G], turned(q), ACT.Gelu,
                                     scale=vec[:, g0 + c:g0 + c + 1],
                                     bias=vec[:, b0 + c:b0 + c + 1]).then_inc(s_ge, 1)
            act.wait_ge(s_w3, 1)
            nc.scalar.activation(y_cols[:, :], pH[:, 0:NT], ACT.Sigmoid, bias=b3[:, 0:1]).then_inc(s_yc, 1)

        @block.vector
        def _(dve):
            v = Steps(dve, s_dve)
            dve.sem_inc(s_slot, RING)
            dve.sem_inc(s_ah, 1)
            dve.sem_inc(s_scr, 1)
            dve.wait_ge(s_idx, 32)
            for g in range(NG):
                nc.vector.tensor_copy(
                    idx_c[:, g * CPG:(g + 1) * CPG, :].rearrange("p c (t s) -> p c t s", t=2),
                    idx[:, 2 * g:2 * g + 2, :].rearrange("p t (c s) -> p c t s", s=CH)).then_inc(s_idc, 1)
            v.done(nc.vector.memset(ones[:, :], 1.0))
            v.done(nc.vector.memset(squeeze[:, :], 1.0))
            dve.wait_ge(s_idc, NG)
            nc.vector.tensor_copy(idx_g[:, :, :], idx_c[:, 0:RING, :]).then_inc(s_idxg, RING)
            v.done(nc.vector.tensor_scalar(kept[:, :, :], idx_c[:, :, :], 0.0, None, ALU.not_equal))
            v.done(nc.vector.tensor_scalar(masked[:, :, :], idx_c[:, :, :], 0.0, MASKED, ALU.is_equal, ALU.mult))
            dve.wait_ge(s_small, 16 * len(SMALL))
            v.done(nc.vector.tensor_copy(levels_f[:, :, :], levels_i[:, :, :]))
            v.wait()
            v.done(nc.vector.tensor_scalar(one_hot[:, :, :], levels_f[:, :, :], iota[:, 0:1], None, ALU.is_equal))
            ONE_HOT = v.n
            v.done(nc.vector.tensor_tensor(w_u[:, :], aw1[:, 0, :], aw1[:, 2, :], ALU.add))
            v.done(nc.vector.tensor_tensor(w_s[:, :], aw1[:, 1, :], aw1[:, 2, :], ALU.subtract))
            v.done(nc.vector.tensor_copy(w_p[:, :], aw1[:, 3, :]))
            dve.wait_ge(s_pro, 3)
            for t in range(NT):
                v.done(nc.vector.bn_stats(stats[:, t, :], pH[:, t * D:(t + 1) * D]))
            v.wait()
            for t in range(NT):
                v.done(nc.vector.bn_aggr(moments[:, t, :], stats[:, t, :]))
            v.wait()
            nc.vector.tensor_scalar(spread[:, :], moments[:, :, 1], EPS, None, ALU.add).then_inc(s_sqrt, 1)
            dve.wait_ge(s_sqrt, 2)
            v.done(nc.vector.reciprocal(spread[:, :], spread[:, :]))
            v.wait()
            for t in range(NT):
                v.done(nc.vector.tensor_scalar(img_hat[:, t, :], pH[:, t * D:(t + 1) * D], moments[:, t, 0:1],
                                               spread[:, t:t + 1], ALU.subtract, ALU.mult))
            IMG_HAT = v.n
            dve.wait_ge(s_pra, 6)
            v.done(nc.vector.tensor_tensor(target[:, :], fields[:, 2, :], fields[:, 3, :], ALU.add))
            TARGET = v.n
            v.done(nc.vector.tensor_scalar(vec[:, R_CB:R_CB + KT], vec[:, R_CB:R_CB + KT], 1.0, None, ALU.add))
            dve.wait_ge(s_pro, 6)
            v.done(nc.vector.tensor_scalar(u_neg[:, :], pM[:, 0:NG * P], vec[:, R_AB1:R_AB1 + 1], -1.0,
                                           ALU.add, ALU.mult))
            U_NEG = v.n
            dve.wait_ge(s_pro, 7)
            v.done(nc.vector.tensor_scalar(c_row[:, :], pA[:, 0:NT], -1.0, ab2[:, 0:1], ALU.mult, ALU.add))
            v.wait()
            PRO.update(one_hot=ONE_HOT, img_hat=IMG_HAT, target=TARGET, u_neg=U_NEG)
            for g in range(NG):
                v.done(nc.vector.tensor_tensor(
                    shift[:, g * CPG:(g + 1) * CPG, :].rearrange("p c (t s) -> p c t s", t=2),
                    kept[:, g * CPG:(g + 1) * CPG, :].rearrange("p c (t s) -> p c t s", t=2),
                    c_row[:, 2 * g:2 * g + 2].unsqueeze(1).unsqueeze(3).broadcast_to([P, CPG, 2, CH]), ALU.mult))
            v.wait()
            v.done(nc.vector.tensor_tensor(shift[:, :, :], shift[:, :, :], masked[:, :, :], ALU.add))

            def start_group():
                v.done(nc.vector.memset(logit[:, 0, :, CH:CH + 1], LEAST))
                v.done(nc.vector.memset(total[:, :], 0.0))
                v.done(nc.vector.memset(hist[:, :, :], 0.0))
                v.wait()

            def chunk_product(n, g):
                dve.wait_ge(s_st, n + 2)
                nc.vector.tensor_tensor(
                    p_t[:, :].rearrange("p (t s b) -> p t s b", t=2, b=P),
                    s_t[:, :].rearrange("p (t s b) -> p t s b", t=2, b=P),
                    target[:, g * G:(g + 1) * G].rearrange("p (t b) -> p t b", t=2).unsqueeze(2)
                    .broadcast_to([P, 2, CH, P]), ALU.mult).then_inc(s_pt, 1)

            def next_indices(n, r):
                nc.vector.tensor_copy(idx_g[:, r, :],
                                      idx_c[:, bass.ds(n + RING, 1), :].rearrange("p a s -> p (a s)"))\
                    .then_inc(s_idxg, 1)

            def chunk_relu(n, g):
                dve.wait_ge(s_h, n + 2)
                dve.wait_ge(s_sc, n + 1)
                nc.vector.tensor_tensor(
                    act_h[:, :].rearrange("p (s b) -> p s b", b=P), pH[:, 0:HALF_C].rearrange("p (s b) -> p s b", b=P),
                    u_neg[:, g * P:(g + 1) * P].unsqueeze(1).broadcast_to([P, CH, P]), ALU.max).then_inc(s_ah, 1)

            def chunk_max(n, r):
                dve.wait_ge(s_sc, n + 2)
                now, then = logit[:, r, :, :], logit[:, (r + 1) % RING, :, :]
                nc.vector.tensor_tensor(now[:, :, 0:CH], pM[:, 0:CW].rearrange("p (t s) -> p t s", t=2),
                                        kept[:, bass.ds(n, 1), :].rearrange("p a (t s) -> p (a t) s", t=2),
                                        ALU.mult).then_inc(s_scr, 1)
                dve.wait_ge(s_scr, n + 2)
                v.done(nc.vector.tensor_tensor(now[:, :, 0:CH], now[:, :, 0:CH],
                                               shift[:, bass.ds(n, 1), :].rearrange("p a (t s) -> p (a t) s", t=2),
                                               ALU.add))
                v.wait()
                v.done(nc.vector.tensor_reduce(then[:, :, CH:CH + 1], now, AX_X, ALU.max))
                v.wait()
                nc.vector.tensor_tensor(diff[:, :, :], now, then[:, :, CH:CH + 1].broadcast_to([P, 2, CH + 1]),
                                        ALU.subtract).then_inc(s_dif, 1)

            def chunk_rows(n):
                dve.wait_ge(s_exp, n + 1)
                v.done(nc.vector.tensor_tensor(total[:, :], total[:, :], exps[:, :, CH], ALU.mult))
                v.done(nc.vector.tensor_reduce(part_sum[:, :], exps[:, :, 0:CH], AX_X, ALU.add))
                v.wait()
                v.done(nc.vector.tensor_tensor(total[:, :], total[:, :], part_sum[:, :], ALU.add))
                dve.wait_ge(s_wgh, n - CPG + 1)
                for at, w in ((1, 2), (1, 1)):
                    v.done(nc.vector.tensor_tensor(weighed[:, at:at + w, :, :], weighed[:, at:at + w, :, :],
                                                   weighed[:, at + w:at + 2 * w, :, :], ALU.add))
                    t = at + w - 2
                    v.done(nc.vector.scalar_tensor_tensor(
                        out=hist[:, t, :], in0=hist[:, t, :], scalar=exps[:, t, CH:CH + 1],
                        in1=weighed[:, 0, t, :], op0=ALU.mult, op1=ALU.add))
                    v.wait(1)
                v.wait()
                v.done(nc.vector.tensor_tensor(hist[:, :, :], hist[:, :, :], weighed[:, 1, :, :], ALU.add))

            def chunk_rows_alone(n, r):
                dve.wait_ge(s_exp, n + 1)
                v.done(nc.vector.tensor_tensor(hist[:, :, :], hist[:, :, :],
                                               exps[:, :, CH:CH + 1].broadcast_to([P, 2, D]), ALU.mult))
                v.done(nc.vector.tensor_tensor(total[:, :], total[:, :], exps[:, :, CH], ALU.mult))
                v.done(nc.vector.tensor_reduce(part_sum[:, :], exps[:, :, 0:CH], AX_X, ALU.add))
                v.wait()
                v.done(nc.vector.tensor_tensor(total[:, :], total[:, :], part_sum[:, :], ALU.add))
                for q in range(CW):
                    s, t = q // 2, q % 2
                    v.wait(1)
                    v.done(nc.vector.scalar_tensor_tensor(
                        out=hist[:, t, :], in0=seq[:, r, t, s, :], scalar=exps[:, t, s:s + 1],
                        in1=hist[:, t, :], op0=ALU.mult, op1=ALU.add))
                v.wait()
                dve.sem_inc(s_slot, 1)

            def end_group(g):
                v.wait()
                v.done(nc.vector.reciprocal(total[:, :], total[:, :]))
                v.wait()
                nc.vector.tensor_tensor(hist[:, :, :], hist[:, :, :],
                                        total[:, :].unsqueeze(2).broadcast_to([P, 2, D]), ALU.mult)\
                    .then_inc(s_hist, 1)

            def lo_part(to, of, hi):
                return nc.vector.tensor_tensor(to, of, hi, ALU.subtract)

            def squeezed(g):
                dve.wait_ge(s_sq, g + 1)
                nc.vector.tensor_scalar(squeeze[0:SE, :], pH[0:SE, 0:G], se_b1[:, 0:1], 0.0,
                                        ALU.add, ALU.max).then_inc(s_sqr, 1)

            def gated(g):
                dve.wait_ge(s_gr, g + 1)
                nc.vector.tensor_tensor(se[:, :, :], fields[:, :, g * G:(g + 1) * G], gate[:, :, :],
                                        ALU.mult).then_inc(s_se, 1)

            def gated_lo(g):
                dve.wait_ge(s_dh, NF * g + 1)
                lo_part(xd[:, g, 1, 0:NF, :], se[:, :, :], f32(xd[:, g, 0, 0:NF, :])).then_inc(s_dl, 1)

            def products(g, steps):
                for i in steps:
                    if i < NV:
                        dve.wait_ge(s_vid, 2 * g + i // 2 + 1)
                        if i >= 2:
                            dve.wait_ge(s_dl, NF * g + i)
                        nc.vector.tensor_tensor(
                            prod[:, i % 2, 0:(NV - i) * G].rearrange("p (k n) -> p k n", n=G),
                            pH[:, i * G:(i + 1) * G].unsqueeze(1).broadcast_to([P, NV - i, G]), se[:, i + 1:NF, :],
                            ALU.mult).then_inc(s_pr, 1)
                    if i:
                        at, w = PARTS[i], NV - i + 1
                        dve.wait_ge(s_dh, NF * g + i + 1)
                        lo_part(xd[:, g, 1, at:at + w, :],
                                prod[:, (i - 1) % 2, 0:w * G].rearrange("p (k n) -> p k n", n=G),
                                f32(xd[:, g, 0, at:at + w, :])).then_inc(s_dl, 1)

            def split_w(j, n, width=KT * P):
                dve.wait_ge(s_wh, n + 1)
                if not isinstance(n, int) or n >= 2:
                    dve.wait_ge(s_mm, n - 1)
                lo_part(w_lo[:, j, 0:width], w_raw[:, j, 0:width], f32(w_hi[:, j, 0:width])).then_inc(s_wl, 1)

            def whole(m, gs):
                v.done(nc.vector.tensor_tensor(by_group(dn, gs), f32(at_block(xd, 0, m, gs)),
                                               f32(at_block(xd, 1, m, gs)), ALU.add))

            def cross(l, m, j, n, gs):
                w = (gs.stop - gs.start) * G
                dve.wait_ge(s_mm, n + 1)
                v.wait()
                ins = nc.vector.scalar_tensor_tensor(
                    out=xf[:, j, 0:w], in0=pA[:, j * BANK:j * BANK + w], scalar=vec[:, bass.ds(m + l * KT, 1)],
                    in1=dn[:, 0:w], op0=ALU.add, op1=ALU.mult)
                if l:
                    v.done(ins)
                    x = by_group(xf[:, j, :], gs)
                    v.wait()
                    v.done(nc.vector.tensor_tensor(x, x, f32(at_block(xe, 0, m, gs)), ALU.add))
                    v.wait()
                    ins = nc.vector.tensor_tensor(x, x, f32(at_block(xe, 1, m, gs)), ALU.add)
                ins.then_inc(s_xf[j], 1)

            def cross_lo(to, m, j, n, gs):
                dve.wait_ge(s_xh, n + 1)
                lo_part(at_block(to, 1, m, gs), by_group(xf[:, j, :], gs), f32(at_block(to, 0, m, gs)))\
                    .then_inc(s_xl, 1)

            def next_whole(j, turn, m, gs):
                dve.wait_ge(s_xf[j], turn + 1)
                whole(m, gs)

            dve.wait_ge(s_late, 16 * len(LATE))
            v.done(nc.vector.tensor_scalar(se1[:, :], se1_in[:, :], 1.0 / D, None, ALU.mult))
            nc.vector.tensor_copy(se2[:, :, :], se2_in[:, :].unsqueeze(2).broadcast_to([SE + 1, NF, P]))\
                .then_inc(s_hist, 1)
            start_group()
            with dve.Fori(0, CPG // RING) as i:
                v.enter(i, RING * (CW + 6))
                for r in range(RING):
                    n = i * RING + r
                    if r == 0:
                        chunk_product(n, 0)
                    chunk_relu(n, 0)
                    next_indices(n, r)
                    if r + 1 < RING:
                        chunk_product(n + 1, 0)
                    chunk_max(n, r)
                    chunk_rows_alone(n, r)
                v.leave(CPG // RING)
            end_group(0)
            chunk_product(CPG, 1)
            dve.wait_ge(s_ht, 1)
            start_group()
            squeezed(0)
            next_indices(CPG, 0)
            split_w(0, 0)
            gated(0)
            chunk_relu(CPG, 1)
            gated_lo(0)
            products(0, range(NV + 1))
            chunk_product(CPG + 1, 1)
            split_w(1, 1)
            chunk_max(CPG, 0)
            dve.wait_ge(s_dl, NF)
            whole(0, groups(0))

            def after(n):
                gs = groups(n)
                cross(0, n, n % 2, n, gs)
                split_w(n % 2, n + 2)
                cross_lo(xe, n, n % 2, n, gs)
                if n + 1 < KT:
                    next_whole(n % 2, n // 2, n + 1, gs)

            for c in range(1, CPG):
                n, r, gs = CPG + c, c % RING, groups(0)
                chunk_relu(n, 1)
                if c < RING:
                    next_indices(n, r)
                chunk_rows(n - 1)
                cross(0, c - 1, (c - 1) % 2, c - 1, gs)
                chunk_max(n, r)
                cross_lo(xe, c - 1, (c - 1) % 2, c - 1, gs)
                next_whole((c - 1) % 2, (c - 1) // 2, c, gs)
                if c + 1 < CPG:
                    chunk_product(n + 1, 1)
                split_w((c + 1) % 2, c + 1)
            chunk_rows(NG * CPG - 1)
            end_group(1)
            after(CPG - 1)
            after(CPG)
            squeezed(1)
            after(CPG + 1)
            gated(1)
            gated_lo(1)
            after(CPG + 2)
            products(1, range(0, 3))
            after(CPG + 3)
            products(1, range(3, NV + 1))
            after(CPG + 4)

            gs = groups(L0B)
            dve.wait_ge(s_dl, NG * NF)
            next_whole((L0B - 1) % 2, (L0B - 1) // 2, 0, gs)
            cross(0, 0, 1, L0B, gs)
            split_w(1, L0B + 2)
            cross_lo(xe, 0, 1, L0B, gs)
            with dve.Fori(0, KT // 2) as i:
                v.enter(i, 2)
                for j in range(2):
                    n, m = 2 * i + j + L0B + 1, 2 * i + j + 1
                    next_whole(1 - j, i + L0B // 2 + j, m, gs)
                    cross(0, m, j, n, gs)
                    split_w(j, n + 2)
                    cross_lo(xe, m, j, n, gs)
                v.leave(KT // 2)
            gs = groups(L1)
            with dve.Fori(0, KT // 2 - 1) as i:
                v.enter(i, 6)
                for j in range(2):
                    n, m = 2 * i + j + L1, 2 * i + j
                    next_whole(1 - j, i + L1 // 2 - (1 - j), m, gs)
                    cross(1, m, j, n, gs)
                    split_w(j, n + 2)
                    cross_lo(xd, m, j, n, gs)
                v.leave(KT // 2 - 1)
            for n in range(MLP0 - 3, ITEMS - 2):
                if n < MLP0:
                    next_whole((n - 1) % 2, (n - 1) // 2, n - L1, gs)
                    cross(1, n - L1, n % 2, n, gs)
                split_w(n % 2, n + 2, KT * P if n + 2 < MLP0 else W1K * N1)
                if n < MLP0:
                    cross_lo(xd, n - L1, n % 2, n, gs)

            def hat_rows(l, t, acc, hat):
                dve.wait_ge(s_pow, l * NT + t + 1)
                nc.vector.tensor_scalar(hat[:, t, :], acc(t), moments[:, t, 0:1], spread[:, t:t + 1],
                                        ALU.subtract, ALU.mult).then_inc(s_hat, 1)

            for l, (ready, acc, hat) in enumerate(((s_w1, first_acc, hat1), (s_w2, second_acc, hat2))):
                if l:
                    dve.wait_ge(s_hat, NT)
                for t in range(NT):
                    if l and t == 2:
                        hat_rows(l, t - 1, acc, hat)
                    dve.wait_ge(ready, t + 1)
                    v.done(nc.vector.bn_stats(stats[:, t, :], acc(t)))
                    v.wait()
                    v.done(nc.vector.bn_aggr(moments[:, t, :], stats[:, t, :]))
                    v.wait()
                    nc.vector.tensor_scalar(spread[:, t:t + 1], moments[:, t, 1:2], EPS, None, ALU.add)\
                        .then_inc(s_var, 1)
                    if t and not (l and t == 2):
                        hat_rows(l, t - 1, acc, hat)
                hat_rows(l, NT - 1, acc, hat)
            dve.wait_ge(s_yt, 1)
            nc.vector.tensor_copy(y[:, :], pT[0:NT, 2 * BANK:2 * BANK + P]).then_inc(s_y, 1)

        @block.tensor
        def _(pe):
            mm, tr = nc.tensor.matmul, nc.tensor.transpose
            pe.sem_inc(s_h, 1)
            pe.sem_inc(s_sc, 1)
            pe.wait_ge(s_small, 16 * len(SMALL))
            for t in range(NT):
                ins = tr(pT[:, t * P:(t + 1) * P], emb[:, t, :], ident[:, :])
            ins.then_inc(s_pro, 1)
            tr(pM[:, 0:NR], vec_rows[:, :], ident[0:NR, 0:NR])
            pe.wait_ge(s_dve, PRO["one_hot"])
            for j in range(2):
                ins = mm(pT[:, (1 + j) * BANK:(1 + j) * BANK + B], cate[:, :], one_hot[:, j, :], start=True, stop=True)
            ins.then_inc(s_pro, 1)
            pe.wait_ge(s_pra, 1)
            for t in range(NT):
                mm(pH[:, t * D:(t + 1) * D], ones[0:1, :], mm_b[0:1, :], start=True, stop=False)
                ins = mm(pH[:, t * D:(t + 1) * D], emb_t[:, t, :], mm_w[:, :], start=False, stop=True)
            ins.then_inc(s_pro, 1)
            pe.wait_ge(s_idr, 16 * NT)
            for t in range(NT):
                ins = tr(pT[:, t * P:(t + 1) * P], id_rows[:, t, :], ident[:, :])
            ins.then_inc(s_pro, 1)
            pe.wait_ge(s_dve, PRO["img_hat"])
            pe.wait_ge(s_pra, 4)
            for t in range(NT):
                ins = tr(pT[:, BANK + t * P:BANK + (t + 1) * P], img_hat[:, t, :], ident[:, :])
            ins.then_inc(s_pro, 1)
            pe.wait_ge(s_dve, PRO["target"])
            for t in range(NT):
                h, g = t % 2, t // 2
                ins = mm(pM[h * HID:(h + 1) * HID, g * P:(g + 1) * P], w_u[:, :], target[:, t * P:(t + 1) * P],
                         start=True, stop=True)
            ins.then_inc(s_pro, 1)
            pe.wait_ge(s_dve, PRO["u_neg"])
            for g in range(NG):
                ins = mm(pA[:, 2 * g:2 * g + 2], u_neg[:, g * P:(g + 1) * P], vec[:, R_AW2:R_AW2 + 2],
                         start=True, stop=True)
            ins.then_inc(s_pro, 1)

            def chunk_turn(n, r, turn):
                pe.wait_ge(s_rows[r], 16 * CW * (turn + 1))
                pe.wait_ge(s_st, n + 1)
                for q in range(CW):
                    ins = tr(pT[:, q * P:(q + 1) * P], seq[:, r, q // CH, q % CH, :], ident[:, :])
                ins.then_inc(s_tr, 1)

            def chunk_hidden(n):
                for w, x in ((w_s, s_t), (w_p, p_t)):
                    if w is w_s:
                        pe.wait_ge(s_st, n + 2)
                        pe.wait_ge(s_ah, n + 1)
                    else:
                        pe.wait_ge(s_pt, n + 1)
                    for s0, ns in ((0, 4), (4, CH - 4)):
                        for h in range(2):
                            at = (h * CH + s0) * P
                            ins = mm(pH[h * HID:(h + 1) * HID, s0 * P:(s0 + ns) * P], w[:, :],
                                     x[:, at:at + ns * P], start=(w is w_s), stop=(w is w_p))
                ins.then_inc(s_h, 1)

            def chunk_scores(n):
                pe.wait_ge(s_ah, n + 2)
                pe.wait_ge(s_scr, n + 1)
                for s in range(CH):
                    ins = mm(pM[:, s:s + CH + 1:CH], act_h[:, s * P:(s + 1) * P], vec[:, R_AW2:R_AW2 + 2],
                             start=True, stop=True)
                ins.then_inc(s_sc, 1)

            def hist_turn(g):
                pe.wait_ge(s_hist, g + 2)
                for t in range(2):
                    ins = tr(pM[:, t * P:(t + 1) * P], hist[:, t, :], ident[:, :])
                ins.then_inc(s_ht, 1)

            def squeeze_sum(g, fs):
                if fs.start == 0:
                    pe.wait_ge(s_hist, 1)
                    pe.wait_ge(s_ah, CPG * (g + 1) + 1)
                if fs.stop == NF:
                    pe.wait_ge(s_hc, g + 1)
                for f in fs:
                    ins = mm(pH[0:SE, 0:G], se1[:, f * SE:(f + 1) * SE], fields[:, f, g * G:(g + 1) * G],
                             start=(f == 0), stop=(f == NF - 1))
                if fs.stop == NF:
                    ins.then_inc(s_sq, 1)

            def gate_sum(g):
                pe.wait_ge(s_sqr, g + 1)
                pe.wait_ge(s_st, CPG + 2 if g == 0 else NG * CPG + 1)
                for f in range(NF):
                    ins = mm(pT[:, f * G:(f + 1) * G], se2[:, f, :], squeeze[:, :], start=True, stop=True)
                ins.then_inc(s_ga, 1)

            def vids(g):
                pe.wait_ge(s_ah, CPG + 2 if g == 0 else NG * CPG + 1)
                pe.wait_ge(s_se, g + 1)
                for f in range(NV):
                    ins = mm(pH[:, f * G:(f + 1) * G], bil_w[:, f, :], se[:, f, :], start=True, stop=True)
                    if f % 2:
                        ins.then_inc(s_vid, 1)

            def block(j, x, n, gs, ks, turn, last_lo=None, parts=None):
                if ks.start == 0:
                    pe.wait_ge(s_wl, n + 1)
                    if not isinstance(n, int) or n >= 2:
                        pe.wait_ge(s_xf[j], turn)
                acc = by_group(pA[:, j * BANK:(j + 1) * BANK], gs)
                for k in ks:
                    if last_lo and k == KT - 1:
                        pe.wait_ge(s_xl, last_lo)
                    if parts is not None and k in PARTS:
                        pe.wait_ge(s_dl, NF * parts + PARTS.index(k) + 1)
                    hi, lo = w_hi[:, j, k * P:(k + 1) * P], w_lo[:, j, k * P:(k + 1) * P]
                    mm(acc, hi, x[:, gs, 0, k, :], start=(k == 0), stop=False)
                    mm(acc, hi, x[:, gs, 1, k, :], start=False, stop=False)
                    ins = mm(acc, lo, x[:, gs, 0, k, :], start=False, stop=(k == KT - 1))
                if ks.stop == KT:
                    ins.then_inc(s_mm, 1)

            ALL, CUT = range(KT), KT // 4
            KNOWN, HIST = range(0, NF - 1), range(NF - 1, NF)
            with pe.Fori(0, CPG // RING) as i:
                for r in range(RING):
                    n = i * RING + r
                    if r == 0:
                        chunk_turn(n, r, i)
                    chunk_hidden(n)
                    if r + 1 < RING:
                        chunk_turn(n + 1, r + 1, i)
                    chunk_scores(n)
            chunk_turn(CPG, 0, CPG // RING)
            squeeze_sum(0, KNOWN)
            hist_turn(0)
            squeeze_sum(0, HIST)
            gate_sum(0)
            chunk_hidden(CPG)
            vids(0)
            chunk_scores(CPG)
            pe.wait_ge(s_gr, 1)
            chunk_turn(CPG + 1, 1, CPG // RING)
            gs = groups(0)
            block(0, xd, 0, gs, ALL, 0, parts=0)
            for c in range(1, CPG):
                chunk_hidden(CPG + c)
                block(c % 2, xd, c, gs, range(0, CUT), c // 2)
                chunk_scores(CPG + c)
                if c + 1 < CPG:
                    chunk_turn(CPG + c + 1, (c + 1) % RING, (CPG + c + 1) // RING)
                block(c % 2, xd, c, gs, range(CUT, KT), c // 2)
            squeeze_sum(1, KNOWN)
            for q in range(KT - CPG):
                if q == 0:
                    block(0, xd, CPG, gs, ALL, CPG // 2)
                    hist_turn(1)
                if q == 1:
                    block(1, xd, CPG + 1, gs, range(0, CUT), (CPG + 1) // 2)
                    squeeze_sum(1, HIST)
                    block(1, xd, CPG + 1, gs, range(CUT, KT), (CPG + 1) // 2)
                    gate_sum(1)
                if q >= 2:
                    block((CPG + q) % 2, xd, CPG + q, gs, ALL, (CPG + q) // 2)
                if q == 2:
                    vids(1)

            def b1_rows(t):
                mm(first_acc(t), ones[0:1, :], b1[0:1, :], start=True, stop=False)

            gs = groups(L0B)
            pe.wait_ge(s_gr, NG)
            b1_rows(0)
            block(1, xd, L0B, gs, ALL, L0B // 2, parts=1)
            b1_rows(1)
            with pe.Fori(0, KT // 2) as i:
                for j in range(2):
                    block(j, xd, 2 * i + j + L0B + 1, gs, ALL, i + (L0B + 1) // 2)
            gs = groups(L1)
            b1_rows(2)
            b1_rows(3)
            pe.wait_ge(s_xl, L1 - 1)
            block(0, xe, L1, gs, ALL, L1 // 2, last_lo=L1)
            with pe.Fori(0, KT // 2) as i:
                for j in range(2):
                    block(1 - j, xe, 2 * i + j + L1 + 1, gs, ALL, i + (L1 + 1 + j) // 2)

            def b2_rows(t):
                mm(second_acc(t), ones[0:1, :], b2[0:1, :], start=True, stop=False)

            for q in range(NW1):
                n = MLP0 + q
                last = q == NW1 - 1
                pe.wait_ge(s_wl, n + 1)
                pe.wait_ge(s_xl, L1 + (q + 1) * W1K)
                order = [(k, t) for t in range(NT) for k in range(W1K)] if last else \
                    [(k, t) for k in range(W1K) for t in range(NT)]
                for k, t in order:
                    hi = w_hi[:, n % 2, k * N1:(k + 1) * N1]
                    lo = w_lo[:, n % 2, k * N1:(k + 1) * N1]
                    kk = q * W1K + k
                    x_hi = xd[:, t // 2, 0, kk, (t % 2) * P:(t % 2) * P + P]
                    x_lo = xd[:, t // 2, 1, kk, (t % 2) * P:(t % 2) * P + P]
                    mm(first_acc(t), x_hi, hi, start=False, stop=False)
                    mm(first_acc(t), x_hi, lo, start=False, stop=False)
                    ins = mm(first_acc(t), x_lo, hi, start=False, stop=(kk == KT - 1))
                    if last and k == W1K - 1:
                        ins.then_inc(s_w1, 1)
                if not last:
                    ins.then_inc(s_mm, 1)
                if q == 0:
                    for j in range(2):
                        pe.wait_ge(s_xf[j], (MLP0 + 1 - j) // 2)
                        b2_rows(j)

            def turn(q):
                l, h, c = GELUS[q]
                pe.wait_ge(s_hat, l * NT + 2 * h + 2)
                if q >= 2:
                    pe.wait_ge(s_ge, q - 1)
                for t in range(2):
                    ins = tr(turned(q)[:, t * P:(t + 1) * P], (hat1, hat2)[l][:, 2 * h + t, c * P:(c + 1) * P],
                             ident[:, :])
                ins.then_inc(s_mt, 1)

            turn(0)
            turn(1)
            for t in (2, 3):
                b2_rows(t)
            for q in range(2 * K1):
                _, h, c = GELUS[q]
                pe.wait_ge(s_ge, q + 1)
                for t in (2 * h, 2 * h + 1):
                    ins = mm(second_acc(t), h1_t[:, c, t * P:(t + 1) * P], w2[:, c, :], start=False,
                             stop=(c == K1 - 1))
                    if c == K1 - 1:
                        ins.then_inc(s_w2, 1)
                turn(q + 2)
            for h in range(2):
                q = 2 * K1 + K2 * h
                if h:
                    for c in range(K2):
                        turn(q + c)
                pe.wait_ge(s_ge, q + K2)
                for t in (2 * h, 2 * h + 1):
                    for c in range(K2):
                        ins = mm(pH[:, t:t + 1], h2_t[:, c, t * P:(t + 1) * P], vec[:, R_W3 + c:R_W3 + c + 1],
                                 start=(c == 0), stop=(c == K2 - 1))
            ins.then_inc(s_w3, 1)
            pe.wait_ge(s_yc, 1)
            tr(pT[0:NT, 2 * BANK:2 * BANK + P], y_cols[:, :], ident[:, :]).then_inc(s_yt, 1)


def kernel(**inputs):
    import numpy as np
    import concourse.bacc as bacc
    from concourse.bass_utils import run_bass_kernel_spmd

    nc = bacc.Bacc("TRN2", target_bir_lowering=False, num_devices=1)
    arrays, aps = {}, {}
    for name in INS:
        arr = np.ascontiguousarray(inputs[name])
        arrays[f"in_{name}"] = arr
        aps[name] = nc.dram_tensor(f"in_{name}", arr.shape, mybir.dt.from_np(arr.dtype), kind="ExternalInput").ap()
    consts = {"ident": np.eye(P, dtype=np.float32),
              "iota": np.arange(inputs['L0_rec_cate_table'].shape[0], dtype=np.float32).reshape(-1, 1)}
    for name, arr in consts.items():
        arrays[f"in_{name}"] = arr
        aps[name] = nc.dram_tensor(f"in_{name}", arr.shape, F32, kind="ExternalInput").ap()
    B = inputs['r_item_id'].shape[0]
    out = nc.dram_tensor("out_y", (B,), F32, kind="ExternalOutput").ap()
    build(nc, aps, aps["ident"], aps["iota"], out)
    r = run_bass_kernel_spmd(nc, [arrays], core_ids=[0])
    return r.results[0]["out_y"]
```
